# Optimizing a Trainium2 kernel written in Bass

```python
import numpy as np
import jax
import jax.numpy as jnp

def _softmax(x, axis=-1):
    return jax.nn.softmax(x, axis=axis)

def _gelu(x):
    return jax.nn.gelu(x, approximate=True)

def _silu(x):
    return jax.nn.silu(x)

def _sigmoid(x):
    return jax.nn.sigmoid(x)

def _layernorm(x, axis=-1, eps=1e-05):
    m = jnp.mean(x, axis=axis, keepdims=True)
    v = jnp.var(x, axis=axis, keepdims=True)
    return (x - m) / jnp.sqrt(v + eps)

def _scatter_add(tgt, idx, src, axis=0):
    return tgt.at[idx].add(src)

def _segment_sum(src, seg, n):
    return jax.ops.segment_sum(src, seg, n)
kernel_name = 'mk_flamingo_gated_d1_seqx_r8_321709'

def setup_inputs(seed: int=0):
    np.random.seed(seed)
    _w = jnp.asarray

    def _rec_inputs():
        import jax
        import jax.numpy as jnp
        _rk = jax.random.key(seed)
        x = 7.22e-05 + 1 * jax.random.normal(jax.random.fold_in(_rk, 1), (8, 128, 128), jnp.float32)
        _lenS = 128 - jax.random.randint(jax.random.fold_in(_rk, 7), (8,), 0, max(1, 128 // 4) + 1, jnp.int32)
        _lenS2 = 128 - jax.random.randint(jax.random.fold_in(_rk, 8), (8,), 0, max(1, 128 // 4) + 1, jnp.int32)
        _ctx_1024P = jax.random.normal(jax.random.fold_in(_rk, 11), (8, 16, 128), jnp.float32)
        _ctx_1024c = jax.random.dirichlet(jax.random.fold_in(_rk, 511), 0.3 * jnp.ones((16,), jnp.float32), (8, 128))
        _ctx_1024t = jnp.einsum('bsk,bkd->bsd', _ctx_1024c, _ctx_1024P)
        _ctx_1024t = _ctx_1024t * jax.lax.rsqrt(jnp.mean(jnp.square(_ctx_1024t)) + 1e-12) * 0.953939
        ctx_1024 = 4.13588e-05 + 0.999923 * (_ctx_1024t + 0.3 * jax.random.normal(jax.random.fold_in(_rk, 611), (8, 128, 128), jnp.float32))
        _g = jax.random.normal(jax.random.fold_in(_rk, 9001), (2, 1), jnp.float32)
        _g = jnp.sign(_g) * jnp.maximum(jnp.abs(_g), 1.0) + (_g == 0) * 1.0
        g_xattn = _g[0]
        g_ffn = _g[1]
        return (x, ctx_1024, g_xattn, g_ffn)
    x, ctx_1024, g_xattn, g_ffn = _rec_inputs()

    def _L0_xattn_setup():
        import jax, jax.numpy as jnp
        import numpy as np
        import math
        B, S, D, H = (4, 256, 128, 16)
        DK = D // H
        key = jax.random.key(seed)
        ks = jax.random.split(key, 11)
        mk = lambda k, shape: jax.random.normal(k, shape, dtype=jnp.float32)
        inp = {'query': mk(ks[0], (B, S, D)), 'key': mk(ks[1], (B, S, D)), 'value': mk(ks[2], (B, S, D)), 'Wq': mk(ks[3], (D, D)) * 0.02, 'bq': jnp.zeros((D,), jnp.float32), 'Wk': mk(ks[4], (D, D)) * 0.02, 'bk': jnp.zeros((D,), jnp.float32), 'Wv': mk(ks[5], (D, D)) * 0.02, 'bv': jnp.zeros((D,), jnp.float32), 'Wo': mk(ks[6], (D, D)) * 0.02, 'bo': jnp.zeros((D,), jnp.float32)}
        return inp
    _L0_xattn_all = _L0_xattn_setup()
    _L0_xattn_in = {k: v for k, v in _L0_xattn_all.items() if k in ('Wq', 'bq', 'Wk', 'bk', 'Wv', 'bv', 'Wo', 'bo')}
    del _L0_xattn_all

    def _L0_ffn_setup():
        import jax, jax.numpy as jnp
        import numpy as np
        B, S, H = (1, 256, 128)
        E = 16
        I = 96
        TOPK = 4
        G = 4
        TOPK_G = 2
        SCALE = 2.5
        N_SHARED = 1

        def _route(x, gate_w, gate_bias):
            n = x.shape[0]
            logits = jnp.einsum('nh,eh->ne', x.astype(jnp.float32), gate_w)
            scores = jax.nn.sigmoid(logits)
            sb = scores + gate_bias
            gs = sb.reshape(n, G, E // G)
            group_scores = jnp.sum(jax.lax.top_k(gs, 2)[0], axis=-1)
            _, gidx = jax.lax.top_k(group_scores, TOPK_G)
            gmask = jnp.sum(jax.nn.one_hot(gidx, G, dtype=sb.dtype), axis=1)
            emask = jnp.repeat(gmask, E // G, axis=-1)
            masked = jnp.where(emask > 0, sb, -jnp.inf)
            _, tidx = jax.lax.top_k(masked, TOPK)
            w = jnp.take_along_axis(scores, tidx, axis=1)
            w = w / (jnp.sum(w, axis=-1, keepdims=True) + 1e-20)
            return (tidx, w * SCALE)
        key = jax.random.key(seed)
        ks = jax.random.split(key, 9)

        def rn(k, shape, scale=0.02):
            return jax.random.normal(k, shape, dtype=jnp.float32) * scale
        return dict(hidden_states=jax.random.normal(ks[0], (B, S, H), dtype=jnp.float32), gate_w=rn(ks[1], (E, H)), gate_bias=jax.random.normal(ks[2], (E,), dtype=jnp.float32) * 0.1, w1=rn(ks[3], (E, I, H)), w2=rn(ks[4], (E, H, I)), w3=rn(ks[5], (E, I, H)), ws1=rn(ks[6], (I * N_SHARED, H)), ws2=rn(ks[7], (H, I * N_SHARED)), ws3=rn(ks[8], (I * N_SHARED, H)))
    _L0_ffn_all = _L0_ffn_setup()
    _L0_ffn_in = {k: v for k, v in _L0_ffn_all.items() if k in ('gate_w', 'gate_bias', 'w1', 'w2', 'w3', 'ws1', 'ws2', 'ws3')}
    del _L0_ffn_all
    return {'x': x, 'ctx_1024': ctx_1024, 'g_xattn': g_xattn, 'g_ffn': g_ffn, 'L0_xattn_Wq': _L0_xattn_in['Wq'], 'L0_xattn_bq': _L0_xattn_in['bq'], 'L0_xattn_Wk': _L0_xattn_in['Wk'], 'L0_xattn_bk': _L0_xattn_in['bk'], 'L0_xattn_Wv': _L0_xattn_in['Wv'], 'L0_xattn_bv': _L0_xattn_in['bv'], 'L0_xattn_Wo': _L0_xattn_in['Wo'], 'L0_xattn_bo': _L0_xattn_in['bo'], 'L0_ffn_gate_w': _L0_ffn_in['gate_w'], 'L0_ffn_gate_bias': _L0_ffn_in['gate_bias'], 'L0_ffn_w1': _L0_ffn_in['w1'], 'L0_ffn_w2': _L0_ffn_in['w2'], 'L0_ffn_w3': _L0_ffn_in['w3'], 'L0_ffn_ws1': _L0_ffn_in['ws1'], 'L0_ffn_ws2': _L0_ffn_in['ws2'], 'L0_ffn_ws3': _L0_ffn_in['ws3']}

def reference(x, ctx_1024, g_xattn, g_ffn, L0_xattn_Wq, L0_xattn_bq, L0_xattn_Wk, L0_xattn_bk, L0_xattn_Wv, L0_xattn_bv, L0_xattn_Wo, L0_xattn_bo, L0_ffn_gate_w, L0_ffn_gate_bias, L0_ffn_w1, L0_ffn_w2, L0_ffn_w3, L0_ffn_ws1, L0_ffn_ws2, L0_ffn_ws3):
    import jax
    import jax.numpy as jnp

    def _L0_xattn_ref(query, key, value, Wq, bq, Wk, bk, Wv, bv, Wo, bo):
        import jax, jax.numpy as jnp
        import numpy as np
        import math
        B, S, D, H = (4, 256, 128, 16)
        DK = D // H
        b, s, d = query.shape
        scale = 1.0 / math.sqrt(DK)

        def proj(x, W, bias):
            return (x @ W.T + bias).reshape(b, s, H, DK).transpose(0, 2, 1, 3)
        q = proj(query, Wq, bq)
        k = proj(key, Wk, bk)
        v = proj(value, Wv, bv)
        scores = jnp.einsum('bhqd,bhkd->bhqk', q, k) * scale
        attn = jax.nn.softmax(scores, axis=-1)
        x = jnp.einsum('bhqk,bhkd->bhqd', attn, v)
        x = x.transpose(0, 2, 1, 3).reshape(b, s, d)
        return x @ Wo.T + bo

    def _L0_ffn_ref(hidden_states, gate_w, gate_bias, w1, w2, w3, ws1, ws2, ws3):
        import jax, jax.numpy as jnp
        import numpy as np
        B, S, H = (1, 256, 128)
        E = 16
        I = 96
        TOPK = 4
        G = 4
        TOPK_G = 2
        SCALE = 2.5
        N_SHARED = 1

        def _route(x, gate_w, gate_bias):
            n = x.shape[0]
            logits = jnp.einsum('nh,eh->ne', x.astype(jnp.float32), gate_w)
            scores = jax.nn.sigmoid(logits)
            sb = scores + gate_bias
            gs = sb.reshape(n, G, E // G)
            group_scores = jnp.sum(jax.lax.top_k(gs, 2)[0], axis=-1)
            _, gidx = jax.lax.top_k(group_scores, TOPK_G)
            gmask = jnp.sum(jax.nn.one_hot(gidx, G, dtype=sb.dtype), axis=1)
            emask = jnp.repeat(gmask, E // G, axis=-1)
            masked = jnp.where(emask > 0, sb, -jnp.inf)
            _, tidx = jax.lax.top_k(masked, TOPK)
            w = jnp.take_along_axis(scores, tidx, axis=1)
            w = w / (jnp.sum(w, axis=-1, keepdims=True) + 1e-20)
            return (tidx, w * SCALE)
        b, s, h = hidden_states.shape
        x = hidden_states.reshape(-1, h)
        tidx, tw = _route(x, gate_w, gate_bias)
        n = x.shape[0]
        combine = jnp.zeros((n, E), x.dtype).at[jnp.arange(n)[:, None], tidx].add(tw)
        g = jnp.einsum('nh,eih->nei', x, w1)
        u = jnp.einsum('nh,eih->nei', x, w3)
        hact = jax.nn.silu(g) * u * combine[:, :, None]
        y = jnp.einsum('nei,ehi->nh', hact, w2)
        shared = jnp.einsum('ni,hi->nh', jax.nn.silu(x @ ws1.T) * (x @ ws3.T), ws2)
        return (y + shared).reshape(b, s, h)
    x = x + jnp.tanh(g_xattn[0]) * _L0_xattn_ref(_layernorm(x, axis=-1), ctx_1024, ctx_1024, L0_xattn_Wq, L0_xattn_bq, L0_xattn_Wk, L0_xattn_bk, L0_xattn_Wv, L0_xattn_bv, L0_xattn_Wo, L0_xattn_bo)
    x = x + jnp.tanh(g_ffn[0]) * _L0_ffn_ref(_layernorm(x, axis=-1), L0_ffn_gate_w, L0_ffn_gate_bias, L0_ffn_w1, L0_ffn_w2, L0_ffn_w3, L0_ffn_ws1, L0_ffn_ws2, L0_ffn_ws3)
    return x

_drawn_inputs = setup_inputs


def setup_inputs(seed=0):
    import zlib

    import numpy as np

    out = dict(_drawn_inputs(seed))
    spreads = {'L0_xattn_bq': (0.0, 0.8),
     'L0_xattn_bk': (0.0, 0.8),
     'L0_xattn_bv': (0.0, 0.457),
     'L0_xattn_bo': (0.0, 0.1)}
    factors = {'ctx_1024': 3.437,
     'L0_xattn_Wq': 8.0,
     'L0_xattn_Wk': 8.0,
     'L0_xattn_Wv': 2.852,
     'L0_ffn_gate_w': 8.0,
     'L0_ffn_gate_bias': 8.0,
     'L0_ffn_w1': 8.0,
     'L0_ffn_w2': 8.0,
     'L0_ffn_w3': 8.0,
     'L0_ffn_ws1': 8.0,
     'L0_ffn_ws2': 8.0,
     'L0_ffn_ws3': 8.0}
    for name, (base, spread) in spreads.items():
        noise = np.random.default_rng([zlib.crc32(name.encode()), seed]).standard_normal(out[name].shape)
        drawn = base * np.exp(spread * noise) if base else spread * noise
        out[name] = jnp.asarray(drawn.astype(out[name].dtype))
    for name, factor in factors.items():
        out[name] = (out[name] * factor).astype(out[name].dtype)
    return out
```

```python
from contextlib import ExitStack

import numpy as np

import concourse.bass as bass
from concourse import mybir

F32 = mybir.dt.float32
F32R = mybir.dt.float32r
BF16 = mybir.dt.bfloat16
ALU = mybir.AluOpType
ACT = mybir.ActivationFunctionType
AX_X = mybir.AxisListType.X

B, S, D = 8, 128, 128
H = 16
DK = D // H
NT = B * S
NHALF = 2
HB = B // NHALF
HT = NT // NHALF
HP = H // 2
NE, NI, NG = 16, 96, 4
EG = NE // NG
TOP_G, TOP_E = 2, 4
SCALE = 2.5
EPS = 1e-5
PARTS = 3
WINDOWS = [(0, 3), (24, 2), (40, 1)]
KROWS = 6 * DK
MROWS = KROWS + PARTS
NBLK = NE * NI // 128 + 1
SENT, MASKED, TAKEN = -3e38, -1e38, 3e38


def rows_of(k):
    return (NE * NI, NE * NI + NI) if k == 0 else ((k - 1) * 128, k * 128)


def flamingo(nc, x, ctxT, g_xattn, g_ffn, WqT, bq, WkT, bk, WvT, bv, WoT, bo,
             gate_wT, gate_bias, w1T, w2T, w3T, out):
    with ExitStack() as stack:
        def sb(name, shape, dt=F32):
            return stack.enter_context(nc.sbuf_tensor(name, shape, dt))

        def sem(name):
            return stack.enter_context(nc.semaphore(name))

        ctx_sb = sb("ctx_sb", [128, NT])
        x_sb = sb("x_sb", [128, B, D])
        xb_sb = sb("xb_sb", [128, B, D])
        xn_sb = sb("xn_sb", [128, B, D])
        xnT = sb("xnT", [128, NT])
        x2_sb = sb("x2_sb", [128, B, D])
        wq_sb, wk_sb, wv_sb = sb("wq_sb", [128, D]), sb("wk_sb", [128, D]), sb("wv_sb", [128, D])
        wo_pad = sb("wo_pad", [128, H // 4, D])
        bq_sb, bk_sb = sb("bq_sb", [128, 1]), sb("bk_sb", [128, 1])
        bv_sb, bo_sb = sb("bv_sb", [128, D]), sb("bo_sb", [128, D])
        gates = sb("gates", [128, 2])
        tg = sb("tg", [128, 2])
        gw_sb, gb_sb = sb("gw_sb", [128, NE]), sb("gb_sb", [128, NE])
        w1_sb, w3_sb = sb("w1_sb", [128, NE * NI + NI]), sb("w3_sb", [128, NE * NI + NI])
        w1hi, w1lo = sb("w1hi", [128, NE * NI + NI], F32R), sb("w1lo", [128, NE * NI + NI], F32R)
        w3hi, w3lo = sb("w3hi", [128, NE * NI + NI], F32R), sb("w3lo", [128, NE * NI + NI], F32R)
        w2_sb = sb("w2_sb", [128, NBLK, D])
        identF, identB = sb("identF", [128, 128]), sb("identB", [128, 128], BF16)
        ones32 = sb("ones32", [128, 32])
        full = {"q": [sb(f"qfull{h}", [128, HT]) for h in range(NHALF)],
                "k": [sb(f"kfull{h}", [128, HT]) for h in range(NHALF)]}
        rest = sb("rest", [128, HT])
        part = {"q": [sb(f"qpart{h}", [128, PARTS, HT], BF16) for h in range(NHALF)],
                "k": [sb(f"kpart{h}", [128, PARTS, HT], BF16) for h in range(NHALF)]}
        QS = [sb(f"QS{h}", [128, HP, HT], BF16) for h in range(NHALF)]
        KS = [sb(f"KS{h}", [128, HP, HT], BF16) for h in range(NHALF)]
        v_pad = sb("v_pad", [128, B, H, 32])
        PT = sb("PT", [128, 2, H, S])
        negmax = sb("negmax", [128, 2, HP])
        maxrest = sb("maxrest", [128, 2, HP])
        maxpart = sb("maxpart", [128, 2, PARTS, HP], BF16)
        mT_sb = sb("mT_sb", [2 * PARTS * HP, 2, S], BF16)
        rden = sb("rden", [128, 4 * S])
        OT = sb("OT", [128, 4 * S])
        stats = sb("stats", [128, B, 6])
        mv = sb("mv", [128, B, 2])
        lnv, rstd = sb("lnv", [128, B]), sb("rstd", [128, B])
        nt = sb("nt", [128, 3, B])
        x2T = sb("x2T", [128, HT])
        x2hi = [sb(f"x2hi{h}", [128, HT], F32R) for h in range(NHALF)]
        x2lo = [sb(f"x2lo{h}", [128, HT], F32R) for h in range(NHALF)]
        eneg = sb("eneg", [128, HB, NE])
        score = sb("score", [128, HB, NE])
        biased = sb("biased", [128, HB, NE])
        pairs = sb("pairs", [128, 2, HB * NG, 2])
        gtop = sb("gtop", [128, 5, HB * NG])
        gcmp = sb("gcmp", [128, 2, HB, NG, NG])
        tri = sb("tri", [128, HB, NG, NG])
        gpen = sb("gpen", [128, 2, HB * NG])
        masked = sb("masked", [128, HB, NE + TOP_E])
        top8 = sb("top8", [128, HB, 8])
        taken = sb("taken", [128, HB, NE + TOP_E])
        wsel = sb("wsel", [128, HB, NE])
        wsum = sb("wsum", [128, 3, HB])
        comb = sb("comb", [128, HB, NE])
        combrest = sb("combrest", [128, HB, NE])
        combpart = sb("combpart", [128, HB, PARTS, NE], BF16)
        combT = [sb(f"combT{h}", [PARTS * NE, HT], BF16) for h in range(NHALF)]
        sel = sb("sel", [PARTS * NE, NE, NI], BF16)
        silu = sb("silu", [128, 2, HT])
        su = sb("su", [128, 2, HT])
        hact = sb("hact", [128, 3, HT])
        yT = sb("yT", [128, HT])
        o_sb = sb("o_sb", [128, NHALF, HB, D])
        scr = {t: [nc.dram_tensor(f"scr_{t}{h}", [H, PARTS, DK, HT], BF16, kind="Internal").ap()
                   for h in range(NHALF)] for t in "qk"}

        ps = stack.enter_context(nc.psum_tensor("ps", [128, 8, 512], F32))

        ctx_in, x_in, xh_in = sem("ctx_in"), sem("x_in"), sem("xh_in")
        wk_in, wq_in, wv_in, wo_in = sem("wk_in"), sem("wq_in"), sem("wv_in"), sem("wo_in")
        ctx2_in = sem("ctx2_in")
        bk_in, bq_in, bv_in, bo_in, g_in = (sem("bk_in"), sem("bq_in"), sem("bv_in"), sem("bo_in"),
                                            sem("g_in"))
        gate_in, w1_in, w3_in, w2_in = sem("gate_in"), sem("w1_in"), sem("w3_in"), sem("w2_in")
        ident_ready, bident_ready, consts = sem("ident_ready"), sem("bident_ready"), sem("consts")
        vpad_zero, wopad_zero, kones = sem("vpad_zero"), sem("wopad_zero"), sem("kones")
        xb_ready, sel_ready = sem("xb_ready"), sem("sel_ready")
        wsplit, pool_step = sem("wsplit"), sem("pool_step")
        tanh_ready = sem("tanh_ready")
        kproj, qproj, vproj = sem("kproj"), sem("qproj"), sem("vproj")
        kfull_ready, qfull_ready = sem("kfull_ready"), sem("qfull_ready")
        ksplit, qsplit = sem("ksplit"), sem("qsplit")
        kscr = [sem(f"kscr{h}") for h in range(NHALF)]
        qscr = [sem(f"qscr{h}") for h in range(NHALF)]
        kstack = [sem(f"kstack{h}") for h in range(NHALF)]
        qstack = [sem(f"qstack{h}") for h in range(NHALF)]
        var_ready, rstd_guess = sem("var_ready"), sem("rstd_guess")
        xn_ready, xnT_ps, xnT_ready = sem("xn_ready"), sem("xnT_ps"), sem("xnT_ready")
        v_ready = sem("v_ready")
        dve_step = sem("dve_step")
        s1_done, max_read = sem("s1_done"), sem("max_read")
        parts_done, mt_done, mt_copied = sem("parts_done"), sem("mt_done"), sem("mt_copied")
        m_in = [sem("m_in0"), sem("m_in1")]
        s2_done, exp_done, pv_done = sem("s2_done"), sem("exp_done"), sem("pv_done")
        norm_done, wo_done, x2_done = sem("norm_done"), sem("wo_done"), sem("x2_done")
        x2T_ps, x2T_copied, x2hi_ready, x2lo_ready = (sem("x2T_ps"), sem("x2T_copied"),
                                                      sem("x2hi_ready"), sem("x2lo_ready"))
        logit_done, eneg_ready, comb_ready = sem("logit_done"), sem("eneg_ready"), sem("comb_ready")
        combT_ps, combT_ready = sem("combT_ps"), sem("combT_ready")
        g_done, u_done, c_done = sem("g_done"), sem("u_done"), sem("c_done")
        silu_done, u_read, h_done, hy_done = (sem("silu_done"), sem("u_read"), sem("h_done"),
                                              sem("hy_done"))
        yT_ready, y_ps, out_ready, out_sent = (sem("yT_ready"), sem("y_ps"), sem("out_ready"),
                                               sem("out_sent"))

        block = stack.enter_context(nc.Block())

        S1B, S2B, OB, DB, YB, MB = 0, 2, 4, 5, 6, 7
        GB, UB, CB = 0, 2, 4

        mT_ps = ps[0:2 * PARTS * HP, DB, 0:S // 2].bitcast(BF16)
        combT_bank = ps[0:PARTS * NE, MB, 0:HT // 2].bitcast(BF16)

        def bank(n, cols=512):
            return ps[:, n, 0:cols]

        def heads(b, c, ph):
            return 64 * ph, range(4 * c, 4 * c + 4)

        def tok(b):
            return b // HB, slice((b % HB) * S, (b % HB + 1) * S)

        def routed(s):
            return s - s // NBLK

        def wait_u_read(eng, s):
            if s >= 0 and s % NBLK:
                eng.wait_ge(u_read, routed(s))
            elif s >= 0:
                eng.wait_ge(h_done, s + 1)

        @block.sync
        def _(sp):
            sp.dma_start(ctx_sb[:, 0:HT], ctxT[:, 0:HT]).then_inc(ctx_in, 16)
            sp.dma_start(x_sb[:, 0:HB, :], x[0:HB].rearrange("b s d -> s b d")).then_inc(x_in, 16)
            sp.dma_start(wv_sb[:, :], WvT).then_inc(wv_in, 16)
            sp.dma_start(ctx_sb[:, HT:NT], ctxT[:, HT:NT]).then_inc(ctx2_in, 16)
            sp.dma_start(x_sb[:, HB:B, :], x[HB:B].rearrange("b s d -> s b d")).then_inc(xh_in, 16)

            def stack_rows(t, h, split_done, scratch, stack_sems, dst):
                sp.wait_ge(split_done, h + 1)
                for p in range(PARTS):
                    at = p if t == "q" else PARTS - 1 - p
                    sp.dma_start(scr[t][h][:, at, :, :], part[t][h][:, p, :]).then_inc(scratch[h], 16)
                sp.wait_ge(scratch[h], 16 * PARTS)
                if t == "k":
                    sp.wait_ge(kones, 2)
                for row, n in WINDOWS:
                    at = 0 if t == "q" else PARTS - n
                    for ph in range(2):
                        src = scr[t][h][HP * ph:HP * ph + HP, at:at + n, :, :]
                        sp.dma_start(dst[h][64 * ph + row:64 * ph + row + n * DK, :, :],
                                     src.rearrange("h p d t -> (p d) h t")).then_inc(stack_sems[h], 16)

            stack_rows("k", 0, ksplit, kscr, kstack, KS)
            stack_rows("q", 0, qsplit, qscr, qstack, QS)
            stack_rows("k", 1, ksplit, kscr, kstack, KS)
            stack_rows("q", 1, qsplit, qscr, qstack, QS)
            for b in range(B):
                h, ts = tok(b)
                sp.wait_ge(mt_copied, b + 1)
                for ph in range(2):
                    n = PARTS * HP
                    sp.dma_start(QS[h][64 * ph + KROWS:64 * ph + MROWS, :, ts],
                                 mT_sb[n * ph:n * ph + n, b % 2, :]).then_inc(m_in[b % 2], 16)
            for h in range(NHALF):
                sp.wait_ge(out_ready, h + 1)
                sp.dma_start(out[HB * h:HB * h + HB].rearrange("b s d -> s b d"),
                             o_sb[:, h, :, :]).then_inc(out_sent, 16)
            sp.wait_ge(out_sent, 16 * NHALF)

        @block.gpsimd
        def _(pool):
            steps = [0]

            def step(ins):
                steps[0] += 1
                ins.then_inc(pool_step, 1)
                pool.wait_ge(pool_step, steps[0])

            step(pool.memset(identF[:, :], 0.0))
            pool.affine_select(out=identF[:, :], in_=identF[:, :], compare_op=ALU.not_equal, fill=1.0,
                               base=0, pattern=[[-1, 128]], channel_multiplier=1).then_inc(ident_ready, 1)
            pool.wait_ge(ident_ready, 1)
            pool.tensor_copy(identB[:, :], identF[:, :]).then_inc(bident_ready, 1)
            pool.dma_start(bv_sb[:, :], bv.partition_broadcast(128)).then_inc(bv_in, 16)
            pool.dma_start(bo_sb[:, :], bo.partition_broadcast(128)).then_inc(bo_in, 16)
            pool.dma_start(gb_sb[:, :], gate_bias.partition_broadcast(128)).then_inc(gate_in, 16)
            pool.dma_start(gw_sb[:, :], gate_wT).then_inc(gate_in, 16)
            pool.memset(KS[1][:, :, :].bitcast(F32), ONES2).then_inc(kones, 1)
            pool.memset(v_pad[:, :, :, :], 0.0).then_inc(vpad_zero, 1)
            pool.memset(wo_pad[:, :, :], 0.0).then_inc(wopad_zero, 1)
            pool.wait_ge(wopad_zero, 1)
            for j in range(4):
                pool.dma_start(wo_pad[32 * j:32 * j + DK, :, :],
                               WoT.rearrange("(g j d) n -> j d g n", j=4, d=DK)[j]).then_inc(wo_in, 16)
            pool.dma_start(w1_sb[:, :], w1T).then_inc(w1_in, 16)
            pool.dma_start(w3_sb[:, :], w3T).then_inc(w3_in, 16)
            pool.dma_start(w2_sb[:, 1:NBLK, :],
                           w2T[0:NE * NI, :].rearrange("(k p) n -> p k n", p=128)).then_inc(w2_in, 16)
            pool.dma_start(w2_sb[0:NI, 0, :], w2T[NE * NI:NE * NI + NI, :]).then_inc(w2_in, 16)
            pool.memset(ones32[:, :], 1.0).then_inc(consts, 1)
            pool.memset(masked[:, :, NE:NE + TOP_E], SENT).then_inc(consts, 1)
            pool.wait_ge(bo_in, 16)
            pool.wait_ge(tanh_ready, 1)
            step(pool.tensor_scalar(bo_sb[:, :], bo_sb[:, :], tg[:, 0:1], None, ALU.mult))
            pool.wait_ge(x_in, 16)
            pool.wait_ge(xh_in, 16)
            pool.tensor_tensor(xb_sb[:, :, :], x_sb[:, :, :],
                               bo_sb[:, :].unsqueeze(1).broadcast_to([128, B, D]),
                               ALU.add).then_inc(xb_ready, 1)
            step(pool.memset(tri[:, :, :, :], 1.0))
            pool.affine_select(out=tri[:, :, :, :], in_=tri[:, :, :, :], compare_op=ALU.is_gt, fill=0.0,
                               base=0, pattern=[[0, HB], [1, NG], [-1, NG]],
                               channel_multiplier=0).then_inc(consts, 1)
            for raw, hi, lo, arrived in ((w1_sb, w1hi, w1lo, w1_in), (w3_sb, w3hi, w3lo, w3_in)):
                pool.wait_ge(arrived, 16)
                step(pool.tensor_copy(hi[:, :], raw[:, :]))
                pool.tensor_tensor(lo[:, :], raw[:, :], hi[:, :].bitcast(F32),
                                   ALU.subtract).then_inc(wsplit, 1)
            step(pool.memset(sel[:, :, :], 0.0))
            for p in range(PARTS):
                ins = pool.affine_select(out=sel[:, :, :], in_=sel[:, :, :], compare_op=ALU.not_equal,
                                         fill=1.0, base=-NE * p, pattern=[[-1, NE], [0, NI]],
                                         channel_multiplier=1)
                if p < PARTS - 1:
                    step(ins)
                else:
                    ins.then_inc(sel_ready, 1)
            for h in range(NHALF):
                pool.wait_ge(x2T_copied, h + 1)
                pool.wait_ge(x2hi_ready, h + 1)
                pool.tensor_tensor(x2lo[h][:, :], x2T[:, :], x2hi[h][:, :].bitcast(F32),
                                   ALU.subtract).then_inc(x2lo_ready, 1)

        @block.scalar
        def _(act):
            act.dma_start(wk_sb[:, :], WkT).then_inc(wk_in, 16)
            act.dma_start(bk_sb[:, :], bk).then_inc(bk_in, 16)
            act.dma_start(gates[:, 0:1], g_xattn.partition_broadcast(128)).then_inc(g_in, 16)
            act.dma_start(gates[:, 1:2], g_ffn.partition_broadcast(128)).then_inc(g_in, 16)
            act.dma_start(wq_sb[:, :], WqT).then_inc(wq_in, 16)
            act.dma_start(bq_sb[:, :], bq).then_inc(bq_in, 16)
            act.wait_ge(g_in, 32)
            act.activation(tg[:, :], gates[:, :], ACT.Tanh).then_inc(tanh_ready, 1)
            act.preload_act_table_set("natural_log_exp_and_others")

            def project_out(t, h, bias, proj_done, bank_no, ready):
                act.wait_ge(proj_done, h + 1)
                act.activation(full[t][h][:, :], bank(bank_no), ACT.Identity, bias=bias[:, :])
                act.activation(part[t][h][:, 0, :], bank(bank_no), ACT.Identity,
                               bias=bias[:, :]).then_inc(ready, 1)

            def guess_rstd(n, cols):
                act.wait_ge(var_ready, n + 1)
                act.activation(lnv[:, cols], nt[:, 0, cols], ACT.Ln).then_inc(rstd_guess, 1)
                act.wait_ge(rstd_guess, 2 * n + 1)
                act.activation(rstd[:, cols], lnv[:, cols], ACT.Exp, scale=-0.5).then_inc(rstd_guess, 1)

            act.wait_ge(bk_in, 16)
            project_out("k", 0, bk_sb, kproj, 0, kfull_ready)
            guess_rstd(0, slice(0, HB))
            project_out("k", 1, bk_sb, kproj, 1, kfull_ready)
            guess_rstd(1, slice(HB, B))
            act.wait_ge(bq_in, 16)
            for h in range(NHALF):
                act.wait_ge(xnT_ps, h + 1)
                act.activation(xnT[:, HT * h:HT * h + HT], bank(2 + h), ACT.Copy).then_inc(xnT_ready, 1)
                project_out("q", h, bq_sb, qproj, 4 + h, qfull_ready)

            def move_maxima(b):
                act.wait_ge(mt_done, b + 1)
                if b >= 2:
                    act.wait_ge(m_in[b % 2], 32 * (b // 2))
                act.activation(mT_sb[:, b % 2, :], mT_ps, ACT.Copy).then_inc(mt_copied, 1)

            def exponentials(b, c):
                act.wait_ge(s2_done, 2 * b + c + 1)
                if b >= 2 and c == 0:
                    act.wait_ge(pv_done, b - 1)
                act.activation(PT[:, b % 2, :, :].rearrange("k (p h) q -> k p h q", p=2)
                               [:, :, 4 * c:4 * c + 4, :].rearrange("k p h q -> k p (h q)"),
                               ps[:, S2B:S2B + 2, :], ACT.Exp, scale=DK ** -0.5).then_inc(exp_done, 1)

            def move_x2T(h):
                act.wait_ge(x2T_ps, h + 1)
                act.activation(x2hi[h][:, :], bank(MB), ACT.Copy).then_inc(x2hi_ready, 1)
                if h:
                    act.wait_ge(x2lo_ready, h)
                    act.wait_ge(logit_done, h)
                act.activation(x2T[:, :], bank(MB), ACT.Copy).then_inc(x2T_copied, 1)

            def sigmoid_exp(h):
                act.wait_ge(logit_done, h + 1)
                act.activation(eneg[:, :, :], ps[:, MB, 0:HB * NE].rearrange("p (t e) -> p t e", e=NE),
                               ACT.Exp, scale=-1.0).then_inc(eneg_ready, 1)

            def move_combT(h):
                act.wait_ge(combT_ps, h + 1)
                act.activation(combT[h][:, :], combT_bank, ACT.Copy).then_inc(combT_ready, 1)

            for i in range(B + 2):
                if i == HB + 2:
                    guess_rstd(2, slice(0, HB))
                if i == HB + 3:
                    move_x2T(0)
                if 1 <= i <= B:
                    exponentials(i - 1, 0)
                if i < B:
                    move_maxima(i)
                if 1 <= i <= B:
                    exponentials(i - 1, 1)
                if i == HB + 3:
                    sigmoid_exp(0)
            guess_rstd(3, slice(HB, B))

            def silus(s):
                r = rows_of(s % NBLK)
                n = r[1] - r[0]
                act.wait_ge(g_done, s + 1)
                wait_u_read(act, s - 2)
                act.activation(silu[0:n, s % 2, :], ps[0:n, GB + s % 2, :],
                               ACT.Silu).then_inc(silu_done, 1)

            def move_yT(h):
                act.wait_ge(hy_done, NBLK * (h + 1))
                if h:
                    act.wait_ge(y_ps, h)
                act.activation(yT[:, :], bank(YB), ACT.Copy).then_inc(yT_ready, 1)

            for s in range(2 * NBLK):
                silus(s)
                if s == 0:
                    move_combT(0)
                if s == X2T_AT:
                    move_x2T(1)
                if s == LOGITS_AT:
                    sigmoid_exp(1)
                if s == COMBT_AT:
                    move_combT(1)
                if s == NBLK + 2:
                    move_yT(0)
            move_yT(1)

        @block.vector
        def _(dve):
            steps = [0]

            def step(ins):
                steps[0] += 1
                ins.then_inc(dve_step, 1)
                dve.wait_ge(dve_step, steps[0])

            dve.memset(KS[0][:, :, :].bitcast(F32), ONES2).then_inc(kones, 1)

            def ln_stats(src, b):
                return dve.bn_stats(stats[:, b, :], src[:, b, :])

            def ln_variance(cols):
                for b in range(cols.start, cols.stop):
                    ins = dve.bn_aggr(mv[:, b, :], stats[:, b, :])
                step(ins)
                dve.tensor_scalar(nt[:, 0, cols], mv[:, cols, 1], EPS, None, ALU.add).then_inc(var_ready, 1)

            def ln_apply(n, src, cols):
                dve.wait_ge(rstd_guess, 2 * n + 2)
                step(dve.tensor_tensor(nt[:, 1, cols], rstd[:, cols], rstd[:, cols], ALU.mult))
                step(dve.tensor_tensor(nt[:, 2, cols], nt[:, 1, cols], nt[:, 0, cols], ALU.mult))
                step(dve.tensor_scalar(nt[:, 1, cols], nt[:, 2, cols], -0.5, 1.5, ALU.mult, ALU.add))
                step(dve.tensor_tensor(nt[:, 2, cols], nt[:, 1, cols], rstd[:, cols], ALU.mult))
                for b in range(cols.start, cols.stop):
                    dve.tensor_scalar(xn_sb[:, b, :], src[:, b, :], mv[:, b, 0:1], nt[:, 2, b:b + 1],
                                      ALU.subtract, ALU.mult).then_inc(xn_ready, 1)

            def split(t, h, ready, done):
                f, r, p = full[t][h], rest, part[t][h]
                dve.wait_ge(ready, h + 1)
                if t == "q":
                    dve.wait_ge(ksplit, h + 1)
                elif h:
                    dve.wait_ge(qsplit, h)
                step(dve.tensor_tensor(r[:, :], f[:, :], p[:, 0, :], ALU.subtract))
                step(dve.tensor_copy(p[:, 1, :], r[:, :]))
                dve.tensor_tensor(p[:, 2, :], r[:, :], p[:, 1, :], ALU.subtract).then_inc(done, 1)

            def move_v(n):
                dve.wait_ge(vproj, n + 1)
                dve.tensor_tensor(
                    v_pad[:, HB * n:HB * n + HB, :, 0:DK],
                    bank(6 + n).rearrange("p (b h d) -> p b h d", b=HB, d=DK),
                    bv_sb[:, :].rearrange("p (h d) -> p h d", d=DK).unsqueeze(1)
                    .broadcast_to([128, HB, H, DK]), ALU.add).then_inc(v_ready, 1)

            lo4, hi4 = slice(0, HB), slice(HB, B)
            dve.wait_ge(x_in, 16)
            for b in range(HB):
                ins = ln_stats(x_sb, b)
            step(ins)
            ln_variance(lo4)
            split("k", 0, kfull_ready, ksplit)
            ln_apply(0, x_sb, lo4)
            dve.wait_ge(xh_in, 16)
            for b in range(HB, B):
                ins = ln_stats(x_sb, b)
            step(ins)
            ln_variance(hi4)
            split("q", 0, qfull_ready, qsplit)
            ln_apply(1, x_sb, hi4)
            split("k", 1, kfull_ready, ksplit)
            dve.wait_ge(bv_in, 16)
            dve.wait_ge(vpad_zero, 1)
            move_v(0)
            split("q", 1, qfull_ready, qsplit)
            move_v(1)

            def maxima(b, c):
                dve.wait_ge(s1_done, 2 * b + c + 1)
                dve.tensor_reduce(negmax[:, :, 4 * c:4 * c + 4],
                                  ps[:, S1B:S1B + 2, :].rearrange("q p (h k) -> q p h k", k=S),
                                  AX_X, ALU.max, negate=True).then_inc(max_read, 1)

            def maxima_parts(b):
                dve.wait_ge(max_read, 2 * b + 2)
                if b:
                    dve.wait_ge(mt_done, b)
                step(dve.tensor_copy(maxpart[:, :, 0, :], negmax[:, :, :]))
                step(dve.tensor_tensor(maxrest[:, :, :], negmax[:, :, :], maxpart[:, :, 0, :],
                                       ALU.subtract))
                step(dve.tensor_copy(maxpart[:, :, 1, :], maxrest[:, :, :]))
                dve.tensor_tensor(maxpart[:, :, 2, :], maxrest[:, :, :], maxpart[:, :, 1, :],
                                  ALU.subtract).then_inc(parts_done, 1)

            def normalize(b):
                dve.wait_ge(pv_done, b + 1)
                step(dve.reciprocal(rden[:, :], bank(DB)))
                if b:
                    dve.wait_ge(wo_done, b)
                dve.tensor_tensor(OT[:, :], bank(OB), rden[:, :], ALU.mult).then_inc(norm_done, 1)

            def residual(b):
                dve.wait_ge(wo_done, b + 1)
                if b == 0:
                    dve.wait_ge(xb_ready, 1)
                dve.scalar_tensor_tensor(x2_sb[:, b, :], bank(YB, D), tg[:, 0:1], xb_sb[:, b, :],
                                         ALU.mult, ALU.add).then_inc(x2_done, 1)
                dve.wait_ge(x2_done, b + 1)
                step(ln_stats(x2_sb, b))

            def route_scores(h):
                dve.wait_ge(eneg_ready, h + 1)
                step(dve.tensor_scalar(eneg[:, :, :], eneg[:, :, :], 1.0, None, ALU.add))
                step(dve.reciprocal(score[:, :, :], eneg[:, :, :]))
                step(dve.tensor_tensor(biased[:, :, :], score[:, :, :],
                                       gb_sb[:, :].unsqueeze(1).broadcast_to([128, HB, NE]), ALU.add))
                by_group = biased[:, :, :].rearrange("p t (g e) -> p (t g) e", e=EG)
                dve.tensor_tensor(pairs[:, 0, :, :], by_group[:, :, 0:2], by_group[:, :, 2:4], ALU.max)
                step(dve.tensor_tensor(pairs[:, 1, :, :], by_group[:, :, 0:2], by_group[:, :, 2:4],
                                       ALU.min))
                dve.tensor_tensor(gtop[:, 0, :], pairs[:, 0, :, 0], pairs[:, 0, :, 1], ALU.max)
                dve.tensor_tensor(gtop[:, 1, :], pairs[:, 0, :, 0], pairs[:, 0, :, 1], ALU.min)
                step(dve.tensor_tensor(gtop[:, 2, :], pairs[:, 1, :, 0], pairs[:, 1, :, 1], ALU.max))
                step(dve.tensor_tensor(gtop[:, 3, :], gtop[:, 1, :], gtop[:, 2, :], ALU.max))
                step(dve.tensor_tensor(gtop[:, 4, :], gtop[:, 0, :], gtop[:, 3, :], ALU.add))

            def route_groups():
                gs = gtop[:, 4, :].rearrange("p (t g) -> p t g", g=NG)
                other = gs.unsqueeze(2).broadcast_to([128, HB, NG, NG])
                own = gs.unsqueeze(3).broadcast_to([128, HB, NG, NG])
                dve.tensor_tensor(gcmp[:, 0, :, :, :], other, own, ALU.is_gt)
                step(dve.tensor_tensor(gcmp[:, 1, :, :, :], other, own, ALU.is_equal))
                step(dve.tensor_tensor(gcmp[:, 1, :, :, :], gcmp[:, 1, :, :, :], tri[:, :, :, :], ALU.mult))
                step(dve.tensor_tensor(gcmp[:, 0, :, :, :], gcmp[:, 0, :, :, :], gcmp[:, 1, :, :, :],
                                       ALU.add))
                step(dve.tensor_reduce(gpen[:, 0, :],
                                       gcmp[:, 0, :, :, :].rearrange("p t g o -> p (t g) o"),
                                       AX_X, ALU.add))
                step(dve.tensor_scalar(gpen[:, 1, :], gpen[:, 0, :], TOP_G - 0.5, MASKED,
                                       ALU.is_ge, ALU.mult))
                step(dve.tensor_tensor(
                    masked[:, :, 0:NE].rearrange("p t (g e) -> p t g e", e=EG),
                    biased[:, :, :].rearrange("p t (g e) -> p t g e", e=EG),
                    gpen[:, 1, :].rearrange("p (t g) -> p t g", g=NG).unsqueeze(3)
                    .broadcast_to([128, HB, NG, EG]), ALU.add))

            def route_top():
                for t in range(HB):
                    ins = dve.max(top8[:, t, :], masked[:, t, :])
                step(ins)
                step(dve.memset(top8[:, :, TOP_E:8], SENT))
                for t in range(HB):
                    ins = dve.match_replace(taken[:, t, :], top8[:, t, :], masked[:, t, :], TAKEN)
                step(ins)

            def route_weights(h):
                step(dve.scalar_tensor_tensor(wsel[:, :, :], taken[:, :, 0:NE], TAKEN / 2,
                                              score[:, :, :], ALU.is_ge, ALU.mult))
                step(dve.tensor_reduce(wsum[:, 0, :], wsel[:, :, :], AX_X, ALU.add))
                step(dve.tensor_scalar(wsum[:, 1, :], wsum[:, 0, :], 1e-20, None, ALU.add))
                step(dve.reciprocal(wsum[:, 2, :], wsum[:, 1, :]))
                step(dve.scalar_tensor_tensor(comb[:, :, :], wsel[:, :, :], SCALE,
                                              wsum[:, 2, :].unsqueeze(2).broadcast_to([128, HB, NE]),
                                              ALU.mult, ALU.mult))
                if h:
                    dve.wait_ge(combT_ps, h)
                step(dve.tensor_copy(combpart[:, :, 0, :], comb[:, :, :]))
                step(dve.tensor_tensor(combrest[:, :, :], comb[:, :, :], combpart[:, :, 0, :],
                                       ALU.subtract))
                step(dve.tensor_copy(combpart[:, :, 1, :], combrest[:, :, :]))
                dve.tensor_tensor(combpart[:, :, 2, :], combrest[:, :, :], combpart[:, :, 1, :],
                                  ALU.subtract).then_inc(comb_ready, 1)

            for i in range(B + 2):
                if i < B:
                    maxima(i, 0)
                if i >= 2:
                    normalize(i - 2)
                if i < B:
                    maxima(i, 1)
                    maxima_parts(i)
                if i >= 2:
                    residual(i - 2)
                if i == HB + 1:
                    ln_variance(lo4)
                if i == HB + 2:
                    dve.wait_ge(xnT_ps, NHALF)
                    ln_apply(2, x2_sb, lo4)
                if i == HB + 4:
                    dve.wait_ge(gate_in, 32)
                    dve.wait_ge(consts, 3)
                    route_scores(0)
                    route_groups()
                    route_top()
                    route_weights(0)
            ln_variance(hi4)
            ln_apply(3, x2_sb, hi4)

            def ffn_step(s):
                k = s % NBLK
                r = rows_of(k)
                n = r[1] - r[0]
                dve.wait_ge(silu_done, s + 1)
                dve.wait_ge(u_done, s + 1)
                if s >= 3:
                    dve.wait_ge(hy_done, s - 2)
                if k == 0:
                    dve.tensor_tensor(hact[0:n, s % 3, :], silu[0:n, s % 2, :], ps[0:n, UB + s % 2, :],
                                      ALU.mult).then_inc(h_done, 1)
                else:
                    if s >= 2:
                        dve.wait_ge(h_done, s - 1)
                    dve.tensor_tensor(su[:, s % 2, :], silu[:, s % 2, :], ps[:, UB + s % 2, :],
                                      ALU.mult).then_inc(u_read, 1)
                    dve.wait_ge(u_read, routed(s))
                    dve.wait_ge(c_done, routed(s))
                    dve.tensor_tensor(hact[:, s % 3, :], su[:, s % 2, :], ps[:, CB + s % 2, :],
                                      ALU.mult).then_inc(h_done, 1)

            def finish(h):
                dve.wait_ge(y_ps, h + 1)
                dve.scalar_tensor_tensor(o_sb[:, h, :, :].rearrange("p b d -> p (b d)"), bank(MB),
                                         tg[:, 1:2],
                                         x2_sb[:, HB * h:HB * h + HB, :].rearrange("p b d -> p (b d)"),
                                         ALU.mult, ALU.add).then_inc(out_ready, 1)

            for s in range(2 * NBLK):
                ffn_step(s)
                if s == LOGITS_AT:
                    route_scores(1)
                if s == LOGITS_AT + 1:
                    route_groups()
                if s == LOGITS_AT + 2:
                    route_top()
                if s == LOGITS_AT + 3:
                    route_weights(1)
                if s == NBLK + 3:
                    finish(0)
            finish(1)

        @block.tensor
        def _(pe):
            def matmul(o, lhsT, rhs, start=True, stop=True):
                return pe.matmul(o, lhsT, rhs, start=start, stop=stop)

            def project(o, w, rhs, done):
                matmul(o, w[:, :], rhs).then_inc(done, 1)

            pe.wait_ge(wk_in, 16)
            pe.wait_ge(ctx_in, 16)
            project(bank(0), wk_sb, ctx_sb[:, 0:HT], kproj)
            pe.wait_ge(ctx2_in, 16)
            project(bank(1), wk_sb, ctx_sb[:, HT:NT], kproj)
            pe.wait_ge(wv_in, 16)

            def project_v(n):
                for b in range(HB * n, HB * n + HB):
                    ins = matmul(ps[:, 6 + n, (b % HB) * D:(b % HB + 1) * D],
                                 ctx_sb[:, b * S:(b + 1) * S], wv_sb[:, :])
                ins.then_inc(vproj, 1)

            project_v(0)
            pe.wait_ge(ident_ready, 1)
            pe.wait_ge(wq_in, 16)
            for h in range(NHALF):
                for b in range(HB * h, HB * h + HB):
                    pe.wait_ge(xn_ready, b + 1)
                    ins = pe.transpose(ps[:, 2 + h, (b % HB) * S:(b % HB + 1) * S], xn_sb[:, b, :],
                                       identF[:, :])
                ins.then_inc(xnT_ps, 1)
                pe.wait_ge(xnT_ready, h + 1)
                project(bank(4 + h), wq_sb, xnT[:, HT * h:HT * h + HT], qproj)
            project_v(1)

            def scores(b, c):
                n = 2 * b + c
                h, ts = tok(b)
                if n == 0:
                    pe.wait_ge(kfull_ready, 2)
                    pe.wait_ge(xnT_ready, 2)
                    pe.wait_ge(kstack[h], 96)
                    pe.wait_ge(qstack[h], 96)
                elif n == 2 * HB:
                    pe.wait_ge(kstack[h], 96)
                    pe.wait_ge(qstack[h], 96)
                if n:
                    pe.wait_ge(max_read, n)
                for i in range(4):
                    for ph in range(2):
                        hp = 4 * c + i
                        rows = slice(64 * ph, 64 * ph + KROWS)
                        ins = matmul(ps[:, S1B + ph, i * S:(i + 1) * S], QS[h][rows, hp, ts],
                                     KS[h][rows, hp, ts])
                ins.then_inc(s1_done, 1)

            def scores_less_max(b, c):
                n = 2 * b + c
                h, ts = tok(b)
                if c == 0:
                    pe.wait_ge(m_in[b % 2], 32 * (b // 2 + 1))
                if n:
                    pe.wait_ge(exp_done, n)
                for i in range(4):
                    for ph in range(2):
                        hp = 4 * c + i
                        rows = slice(64 * ph, 64 * ph + MROWS)
                        ins = matmul(ps[:, S2B + ph, i * S:(i + 1) * S], KS[h][rows, hp, ts],
                                     QS[h][rows, hp, ts])
                ins.then_inc(s2_done, 1)

            def transpose_maxima(b):
                pe.wait_ge(parts_done, b + 1)
                if b == 0:
                    pe.wait_ge(bident_ready, 1)
                    pe.wait_ge(qfull_ready, 2)
                pe.transpose(mT_ps, maxpart[:, :, :, :].rearrange("q p r h -> q (p r h)"),
                             identB[:, :]).then_inc(mt_done, 1)

            def values(b):
                pe.wait_ge(exp_done, 2 * b + 2)
                if b == 0:
                    pe.wait_ge(v_ready, 2)
                    pe.wait_ge(qfull_ready, 2)
                    pe.wait_ge(consts, 1)
                else:
                    pe.wait_ge(norm_done, b)
                pe.wait_ge(mt_copied, min(b + 2, B))
                for g in range(4):
                    for j in range(4):
                        head = 4 * g + j
                        matmul(ps[32 * j:32 * j + 32, OB, g * S:(g + 1) * S], v_pad[:, b, head, :],
                               PT[:, b % 2, head, :])
                for j in range(4):
                    ins = matmul(ps[32 * j:32 * j + 32, DB, :], ones32[:, :], PT[:, b % 2, j:H:4, :])
                ins.then_inc(pv_done, 1)

            def project_out(b):
                pe.wait_ge(norm_done, b + 1)
                if b == 0:
                    pe.wait_ge(wo_in, 64)
                else:
                    pe.wait_ge(x2_done, b)
                for g in range(4):
                    ins = matmul(bank(YB, D), OT[:, g * S:(g + 1) * S], wo_pad[:, g, :],
                                 start=(g == 0), stop=(g == 3))
                ins.then_inc(wo_done, 1)

            def transpose_x2(h):
                if h:
                    pe.wait_ge(combT_ready, h)
                for b in range(HB * h, HB * h + HB):
                    pe.wait_ge(xn_ready, B + b + 1)
                    ins = pe.transpose(ps[:, MB, (b % HB) * S:(b % HB + 1) * S], xn_sb[:, b, :],
                                       identF[:, :])
                ins.then_inc(x2T_ps, 1)

            def logits(h):
                if h == 0:
                    pe.wait_ge(gate_in, 32)
                pe.wait_ge(x2T_copied, h + 1)
                pe.wait_ge(x2hi_ready, h + 1)
                for t in range(HB):
                    ins = matmul(ps[:, MB, t * NE:(t + 1) * NE], x2T[:, t * S:(t + 1) * S], gw_sb[:, :])
                ins.then_inc(logit_done, 1)

            def transpose_comb(h):
                pe.wait_ge(comb_ready, h + 1)
                for t in range(HB):
                    ins = pe.transpose(combT_bank[:, t * S:(t + 1) * S],
                                       combpart[:, t, :, :].rearrange("p r e -> p (r e)"), identB[:, :])
                ins.then_inc(combT_ps, 1)

            for i in range(B + 2):
                if i < B:
                    scores(i, 0)
                if i >= 2:
                    values(i - 2)
                if i < B:
                    scores(i, 1)
                if 1 <= i <= B:
                    scores_less_max(i - 1, 0)
                if i == HB + 3:
                    logits(0)
                if i >= 2:
                    project_out(i - 2)
                if i < B:
                    transpose_maxima(i)
                if 1 <= i <= B:
                    scores_less_max(i - 1, 1)
                if i == HB + 2:
                    transpose_x2(0)

            def split_product(o, hi, lo, r, h):
                cols = slice(*r)
                matmul(o, hi[:, cols], x2hi[h][:, :], stop=False)
                matmul(o, hi[:, cols], x2lo[h][:, :], start=False, stop=False)
                return matmul(o, lo[:, cols], x2hi[h][:, :], start=False)

            def up(s):
                h, k = divmod(s, NBLK)
                r = rows_of(k)
                n = r[1] - r[0]
                if k == 0:
                    pe.wait_ge(x2lo_ready, h + 1)
                if s == 0:
                    pe.wait_ge(wsplit, 2)
                    pe.wait_ge(exp_done, 2 * B)
                if s >= 2:
                    pe.wait_ge(silu_done, s - 1)
                split_product(ps[0:n, GB + s % 2, :], w1hi, w1lo, r, h).then_inc(g_done, 1)
                wait_u_read(pe, s - 2)
                split_product(ps[0:n, UB + s % 2, :], w3hi, w3lo, r, h).then_inc(u_done, 1)
                if s == 0:
                    transpose_comb(0)
                if k:
                    if k == 1:
                        pe.wait_ge(combT_ready, h + 1)
                    if s == 1:
                        pe.wait_ge(sel_ready, 1)
                    if s >= 2:
                        pe.wait_ge(h_done, s - 1)
                    matmul(ps[:, CB + s % 2, :], sel[:, :, :].rearrange("p e i -> p (e i)")[:, slice(*r)],
                           combT[h][:, :]).then_inc(c_done, 1)

            def down(s):
                h, k = divmod(s, NBLK)
                r = rows_of(k)
                n = r[1] - r[0]
                pe.wait_ge(h_done, s + 1)
                if s == 0:
                    pe.wait_ge(w2_in, 32)
                if s == NBLK:
                    pe.wait_ge(yT_ready, 1)
                matmul(bank(YB), w2_sb[0:n, k, :], hact[0:n, s % 3, :], start=(k == 0),
                       stop=(k == NBLK - 1)).then_inc(hy_done, 1)

            def transpose_y(h):
                pe.wait_ge(yT_ready, h + 1)
                if h:
                    pe.wait_ge(out_ready, h)
                for t in range(HB):
                    ins = pe.transpose(ps[:, MB, t * D:(t + 1) * D], yT[:, t * S:(t + 1) * S],
                                       identF[:, :])
                ins.then_inc(y_ps, 1)

            for s in range(2 * NBLK + DOWN_LAG):
                if s < 2 * NBLK:
                    up(s)
                if s >= DOWN_LAG:
                    down(s - DOWN_LAG)
                if s == X2T_AT:
                    transpose_x2(1)
                if s == LOGITS_AT:
                    logits(1)
                if s == COMBT_AT:
                    transpose_comb(1)
                if s == NBLK + 3:
                    transpose_y(0)
            transpose_y(1)


ONES2 = float(np.array([0x3F803F80], np.uint32).view(np.float32)[0])
DOWN_LAG = 2
X2T_AT, LOGITS_AT, COMBT_AT = 0, 2, 7


def kernel(x, ctx_1024, g_xattn, g_ffn, L0_xattn_Wq, L0_xattn_bq, L0_xattn_Wk, L0_xattn_bk,
           L0_xattn_Wv, L0_xattn_bv, L0_xattn_Wo, L0_xattn_bo, L0_ffn_gate_w, L0_ffn_gate_bias,
           L0_ffn_w1, L0_ffn_w2, L0_ffn_w3, L0_ffn_ws1, L0_ffn_ws2, L0_ffn_ws3):
    import concourse.bacc as bacc
    from concourse.bass_utils import run_bass_kernel_spmd

    def lay(a, *axes):
        return np.ascontiguousarray(np.transpose(np.asarray(a), axes))

    def experts_first(w, shared):
        w, shared = np.asarray(w), np.asarray(shared)
        return np.ascontiguousarray(np.concatenate([w.reshape(NE * NI, D), shared], 0).T)

    w2 = np.transpose(np.asarray(L0_ffn_w2), (0, 2, 1)).reshape(NE * NI, D)
    arrays = {
        "x": np.ascontiguousarray(x),
        "ctxT": lay(np.asarray(ctx_1024).reshape(NT, D), 1, 0),
        "g_xattn": np.ascontiguousarray(g_xattn), "g_ffn": np.ascontiguousarray(g_ffn),
        "WqT": lay(L0_xattn_Wq, 1, 0), "bq": np.ascontiguousarray(L0_xattn_bq).reshape(D, 1),
        "WkT": lay(L0_xattn_Wk, 1, 0), "bk": np.ascontiguousarray(L0_xattn_bk).reshape(D, 1),
        "WvT": lay(L0_xattn_Wv, 1, 0), "bv": np.ascontiguousarray(L0_xattn_bv),
        "WoT": lay(L0_xattn_Wo, 1, 0), "bo": np.ascontiguousarray(L0_xattn_bo),
        "gate_wT": lay(L0_ffn_gate_w, 1, 0), "gate_bias": np.ascontiguousarray(L0_ffn_gate_bias),
        "w1T": experts_first(L0_ffn_w1, L0_ffn_ws1),
        "w2T": np.ascontiguousarray(np.concatenate([w2, np.asarray(L0_ffn_ws2).T], 0)),
        "w3T": experts_first(L0_ffn_w3, L0_ffn_ws3),
    }
    nc = bacc.Bacc("TRN2", target_bir_lowering=False, num_devices=1)
    args = [nc.dram_tensor(f"in_{n}", a.shape, mybir.dt.from_np(a.dtype), kind="ExternalInput").ap()
            for n, a in arrays.items()]
    out = nc.dram_tensor("out", (B, S, D), F32, kind="ExternalOutput").ap()
    flamingo(nc, *args, out)
    r = run_bass_kernel_spmd(nc, [{f"in_{n}": a for n, a in arrays.items()}], core_ids=[0])
    return r.results[0]["out"]
```

```python
from contextlib import ExitStack

import numpy as np

import concourse.bass as bass
from concourse import mybir

F32 = mybir.dt.float32
F32R = mybir.dt.float32r
BF16 = mybir.dt.bfloat16
ALU = mybir.AluOpType
ACT = mybir.ActivationFunctionType
AX_X = mybir.AxisListType.X

B, S, D = 8, 128, 128
H = 16
DK = D // H
NT = B * S
NHALF = 2
HB = B // NHALF
HT = NT // NHALF
HP = H // 2
NE, NI, NG = 16, 96, 4
EG = NE // NG
TOP_G, TOP_E = 2, 4
SCALE = 2.5
EPS = 1e-5
PARTS = 3
SLOTS = {"q": (0, 0, 0, 1, 1, 2), "k": (0, 1, 2, 0, 1, 0)}
NS = len(SLOTS["q"])
KROWS = NS * DK
MROWS = KROWS + PARTS
NBLK = NE * NI // 128 + 1
SENT, MASKED, TAKEN = -3e38, -1e38, 3e38


def rows_of(k):
    return (NE * NI, NE * NI + NI) if k == 0 else ((k - 1) * 128, k * 128)


def flamingo(nc, x, k_pack, ctxT1, w_pack, vectors, w13T, w2T, out):
    with ExitStack() as stack:
        def sb(name, shape, dt=F32):
            return stack.enter_context(nc.sbuf_tensor(name, shape, dt))

        def sem(name):
            return stack.enter_context(nc.semaphore(name))

        k_sb = sb("k_sb", [128, D + 2 + HT])
        ctx1_sb = sb("ctx1_sb", [128, HT])
        w_sb = sb("w_sb", [128, 3 * D + NE])
        vec_sb = sb("vec_sb", [128, 2 * D + NE + 2])
        x_sb = sb("x_sb", [128, B, D])
        xb_sb = sb("xb_sb", [128, B, D])
        xn_sb = sb("xn_sb", [128, B, D])
        xnT = sb("xnT", [128, NT])
        x2_sb = sb("x2_sb", [128, B, D])
        wk_sb, bk_sb, bq_sb = k_sb[:, 0:D], k_sb[:, D:D + 1], k_sb[:, D + 1:D + 2]
        ctx_sb = [k_sb[:, D + 2:D + 2 + HT], ctx1_sb[:, :]]
        wq_sb, wv_sb, wo_sb = w_sb[:, 0:D], w_sb[:, D:2 * D], w_sb[:, 2 * D:3 * D]
        gw_sb = w_sb[:, 3 * D:3 * D + NE]
        bv_sb, bo_sb = vec_sb[:, 0:D], vec_sb[:, D:2 * D]
        gb_sb, gates = vec_sb[:, 2 * D:2 * D + NE], vec_sb[:, 2 * D + NE:2 * D + NE + 2]
        tg = sb("tg", [128, 2])
        w13_sb = sb("w13_sb", [128, 2, NE * NI + NI])
        w13hi = sb("w13hi", [128, 2, NE * NI + NI], F32R)
        w13lo = sb("w13lo", [128, 2, NE * NI + NI], F32R)
        w2_sb = sb("w2_sb", [128, NBLK, D])
        w2hi, w2lo = sb("w2hi", [128, NBLK, D], F32R), sb("w2lo", [128, NBLK, D], F32R)
        identF, identB = sb("identF", [128, 128]), sb("identB", [128, 128], BF16)
        full = sb("full", [128, HT])
        rest = sb("rest", [128, HT])
        part = {"q": sb("qpart", [128, NS, HT], BF16), "k": sb("kpart", [128, NS, HT], BF16)}
        QS = [sb(f"QS{h}", [128, HP, HT], BF16) for h in range(NHALF)]
        KS = [sb(f"KS{h}", [128, HP, HT], BF16) for h in range(NHALF)]
        v_pad = sb("v_pad", [128, B, H, 32])
        PT = sb("PT", [128, 2, H, S])
        negmax = sb("negmax", [128, 2, HP])
        maxrest = sb("maxrest", [128, 2, HP])
        maxpart = sb("maxpart", [128, 2, PARTS, HP], BF16)
        mT_sb = sb("mT_sb", [2 * PARTS * HP, 2, S], BF16)
        OA = sb("OA", [128, 4 * S])
        rden = sb("rden", [128, H])
        on_sb = sb("on_sb", [128, H, DK])
        onT = sb("onT", [128, S])
        stats = sb("stats", [128, B, 6])
        mv = sb("mv", [128, B, 2])
        lnv, rstd = sb("lnv", [128, B]), sb("rstd", [128, B])
        nt = sb("nt", [128, 3, B])
        x2T = sb("x2T", [128, HT])
        x2hi = [sb(f"x2hi{h}", [128, HT], F32R) for h in range(NHALF)]
        x2lo = [sb(f"x2lo{h}", [128, HT], F32R) for h in range(NHALF)]
        eneg = sb("eneg", [128, HB, NE])
        score = sb("score", [128, HB, NE])
        biased = sb("biased", [128, HB, NE])
        pairs = sb("pairs", [128, 2, HB * NG, 2])
        gtop = sb("gtop", [128, 5, HB * NG])
        gcmp = sb("gcmp", [128, 2, HB, NG, NG])
        tri = sb("tri", [128, HB, NG, NG])
        gpen = sb("gpen", [128, 2, HB * NG])
        masked = sb("masked", [128, HB, NE + TOP_E])
        top8 = sb("top8", [128, HB, 8])
        taken = sb("taken", [128, HB, NE + TOP_E])
        wsel = sb("wsel", [128, HB, NE])
        wsum = sb("wsum", [128, 3, HB])
        comb = sb("comb", [128, HB, NE])
        combrest = sb("combrest", [128, HB, NE])
        combpart = sb("combpart", [128, HB, PARTS, NE], BF16)
        combT = [sb(f"combT{h}", [PARTS * NE, HT], BF16) for h in range(NHALF)]
        sel = sb("sel", [PARTS * NE, NE, NI], BF16)
        hact = PT[:, 0, 0:12, :].rearrange("p (i c) q -> p i (c q)", i=3)
        silu = PT[:, 1, 0:8, :].rearrange("p (i c) q -> p i (c q)", i=2)
        su = PT[:, 1, 8:16, :].rearrange("p (i c) q -> p i (c q)", i=2)
        hhi, hlo = sb("hhi", [128, 3, HT], F32R), sb("hlo", [128, 3, HT], F32R)
        yT = sb("yT", [128, HT])
        o_sb = xb_sb
        scr = {t: [nc.dram_tensor(f"scr_{t}{h}", [H * DK, NS * HT], BF16, kind="Internal").ap()
                   for h in range(NHALF)] for t in "qk"}

        ps = stack.enter_context(nc.psum_tensor("ps", [128, 8, 512], F32))

        x0_in, x1_in, kp_in, ctx1_in = sem("x0_in"), sem("x1_in"), sem("kp_in"), sem("ctx1_in")
        w_in, vec_in, w13_in, w2_in = sem("w_in"), sem("vec_in"), sem("w13_in"), sem("w2_in")
        ident_ready, bident_ready, consts = sem("ident_ready"), sem("bident_ready"), sem("consts")
        vpad_ready, kones = sem("vpad_ready"), sem("kones")
        xb_ready, sel_ready, wsplit = sem("xb_ready"), sem("sel_ready"), sem("wsplit")
        pool_step, dve_step = sem("pool_step"), sem("dve_step")
        tanh_ready = sem("tanh_ready")
        kproj, qproj, vproj = sem("kproj"), sem("qproj"), sem("vproj")
        proj_moved, slots_ready = sem("proj_moved"), sem("slots_ready")
        scr_out = {t: [sem(f"scr_out_{t}{h}") for h in range(NHALF)] for t in "qk"}
        stacked = {t: [sem(f"stacked_{t}{h}") for h in range(NHALF)] for t in "qk"}
        var_ready, rstd_guess = sem("var_ready"), sem("rstd_guess")
        xn_ready, xnT_ps, xnT_ready = sem("xn_ready"), sem("xnT_ps"), sem("xnT_ready")
        v_ready = sem("v_ready")
        s1_done, max_read = sem("s1_done"), sem("max_read")
        parts_done, mt_done, mt_copied = sem("parts_done"), sem("mt_done"), sem("mt_copied")
        m_in = [sem("m_in0"), sem("m_in1")]
        s2_done, exp_done, pv_done, oa_ready = (sem("s2_done"), sem("exp_done"), sem("pv_done"),
                                                sem("oa_ready"))
        ot_done, on_ready, onT_done, onT_ready = (sem("ot_done"), sem("on_ready"), sem("onT_done"),
                                                  sem("onT_ready"))
        wo_done, x2_done = sem("wo_done"), sem("x2_done")
        x2T_ps, x2T_copied, x2hi_ready, x2lo_ready = (sem("x2T_ps"), sem("x2T_copied"),
                                                      sem("x2hi_ready"), sem("x2lo_ready"))
        logit_done, eneg_ready, comb_ready = sem("logit_done"), sem("eneg_ready"), sem("comb_ready")
        combT_ps, combT_ready = sem("combT_ps"), sem("combT_ready")
        g_done, u_done, c_done = sem("g_done"), sem("u_done"), sem("c_done")
        silu_done, u_read, h_done = sem("silu_done"), sem("u_read"), sem("h_done")
        hhi_done, hlo_done, hy_done = sem("hhi_done"), sem("hlo_done"), sem("hy_done")
        yT_ready, y_ps, out_ready, out_sent = (sem("yT_ready"), sem("y_ps"), sem("out_ready"),
                                               sem("out_sent"))

        block = stack.enter_context(nc.Block())

        S1B, S2B, OB, TB, YB, MB = 0, 2, 4, 5, 6, 7
        GB, UB, CB = 0, 2, 4
        mT_ps = ps[0:2 * PARTS * HP, TB, 0:S // 2].bitcast(BF16)
        combT_bank = ps[0:PARTS * NE, MB, 0:HT // 2].bitcast(BF16)

        def bank(n, cols=512):
            return ps[:, n, 0:cols]

        def tok(b):
            return b // HB, slice((b % HB) * S, (b % HB + 1) * S)

        def routed(s):
            return s - s // NBLK

        def wait_u_read(eng, s):
            if s >= 0 and s % NBLK:
                eng.wait_ge(u_read, routed(s))
            elif s >= 0:
                eng.wait_ge(h_done, s + 1)

        PROJ = [("k", 0), ("q", 0), ("k", 1), ("q", 1)]

        @block.sync
        def _(sp):
            sp.dma_start(x_sb[:, 0:HB, :], x[0:HB].rearrange("b s d -> s b d")).then_inc(x0_in, 16)
            sp.dma_start(k_sb[:, :], k_pack).then_inc(kp_in, 16)
            sp.dma_start(x_sb[:, HB:B, :], x[HB:B].rearrange("b s d -> s b d")).then_inc(x1_in, 16)
            sp.dma_start(ctx1_sb[:, :], ctxT1).then_inc(ctx1_in, 16)

            def spread(n):
                t, h = PROJ[n]
                sp.wait_ge(slots_ready, n + 1)
                sp.dma_start(scr[t][h], part[t][:, :, :].rearrange("p s t -> p (s t)"))\
                    .then_inc(scr_out[t][h], 16)

            def gather(n):
                t, h = PROJ[n]
                dst = QS if t == "q" else KS
                sp.wait_ge(scr_out[t][h], 16)
                if t == "k":
                    sp.wait_ge(kones, 2)
                for ph in range(2):
                    src = scr[t][h][HP * DK * ph:HP * DK * (ph + 1), :]
                    sp.dma_start(dst[h][64 * ph:64 * ph + KROWS, :, :],
                                 src.rearrange("(h d) (s t) -> (d s) h t", d=DK, s=NS)
                                 ).then_inc(stacked[t][h], 16)

            for n in range(len(PROJ)):
                spread(n)
                gather(n)
            for b in range(B):
                h, ts = tok(b)
                sp.wait_ge(mt_copied, b + 1)
                for ph in range(2):
                    n = PARTS * HP
                    sp.dma_start(QS[h][64 * ph + KROWS:64 * ph + MROWS, :, ts],
                                 mT_sb[n * ph:n * ph + n, b % 2, :]).then_inc(m_in[b % 2], 16)
            for h in range(NHALF):
                sp.wait_ge(out_ready, h + 1)
                sp.dma_start(out[HB * h:HB * h + HB].rearrange("b s d -> s b d"),
                             o_sb[:, HB * h:HB * h + HB, :]).then_inc(out_sent, 16)
            sp.wait_ge(out_sent, 16 * NHALF)

        @block.gpsimd
        def _(pool):
            steps = [0]

            def step(ins):
                steps[0] += 1
                ins.then_inc(pool_step, 1)
                pool.wait_ge(pool_step, steps[0])

            step(pool.memset(identF[:, :], 0.0))
            pool.affine_select(out=identF[:, :], in_=identF[:, :], compare_op=ALU.not_equal, fill=1.0,
                               base=0, pattern=[[-1, 128]], channel_multiplier=1).then_inc(ident_ready, 1)
            pool.memset(KS[1][:, :, :].bitcast(F32), ONES2).then_inc(kones, 1)
            pool.wait_ge(ident_ready, 1)
            pool.tensor_copy(identB[:, :], identF[:, :]).then_inc(bident_ready, 1)
            step(pool.memset(v_pad[:, :, :, :], 0.0))
            pool.memset(v_pad[:, :, :, DK:DK + 1], 1.0).then_inc(vpad_ready, 1)
            pool.memset(masked[:, :, NE:NE + TOP_E], SENT).then_inc(consts, 1)
            step(pool.memset(tri[:, :, :, :], 1.0))
            pool.affine_select(out=tri[:, :, :, :], in_=tri[:, :, :, :], compare_op=ALU.is_gt, fill=0.0,
                               base=0, pattern=[[0, HB], [1, NG], [-1, NG]],
                               channel_multiplier=0).then_inc(consts, 1)
            pool.wait_ge(vec_in, 16)
            pool.wait_ge(tanh_ready, 1)
            step(pool.tensor_scalar(bo_sb, bo_sb, tg[:, 0:1], None, ALU.mult))
            pool.wait_ge(x0_in, 16)
            pool.wait_ge(x1_in, 16)
            pool.tensor_tensor(xb_sb[:, :, :], x_sb[:, :, :],
                               bo_sb.unsqueeze(1).broadcast_to([128, B, D]),
                               ALU.add).then_inc(xb_ready, 1)
            for i in range(2):
                pool.wait_ge(w13_in, 16)
                step(pool.tensor_copy(w13hi[:, i, :], w13_sb[:, i, :]))
                pool.tensor_tensor(w13lo[:, i, :], w13_sb[:, i, :], w13hi[:, i, :].bitcast(F32),
                                   ALU.subtract).then_inc(wsplit, 1)
            step(pool.memset(sel[:, :, :], 0.0))
            for p in range(PARTS):
                ins = pool.affine_select(out=sel[:, :, :], in_=sel[:, :, :], compare_op=ALU.not_equal,
                                         fill=1.0, base=-NE * p, pattern=[[-1, NE], [0, NI]],
                                         channel_multiplier=1)
                if p < PARTS - 1:
                    step(ins)
                else:
                    ins.then_inc(sel_ready, 1)
            pool.wait_ge(w2_in, 32)
            pool.tensor_copy(w2hi[0:NI, 0, :], w2_sb[0:NI, 0, :])
            step(pool.tensor_copy(w2hi[:, 1:NBLK, :], w2_sb[:, 1:NBLK, :]))
            pool.tensor_tensor(w2lo[0:NI, 0, :], w2_sb[0:NI, 0, :], w2hi[0:NI, 0, :].bitcast(F32),
                               ALU.subtract)
            pool.tensor_tensor(w2lo[:, 1:NBLK, :], w2_sb[:, 1:NBLK, :],
                               w2hi[:, 1:NBLK, :].bitcast(F32), ALU.subtract).then_inc(wsplit, 1)

            def low_x2(h):
                pool.wait_ge(x2T_copied, h + 1)
                pool.wait_ge(x2hi_ready, h + 1)
                pool.tensor_tensor(x2lo[h][:, :], x2T[:, :], x2hi[h][:, :].bitcast(F32),
                                   ALU.subtract).then_inc(x2lo_ready, 1)

            low_x2(0)
            for s in range(2 * NBLK):
                r = rows_of(s % NBLK)
                n = r[1] - r[0]
                pool.wait_ge(hhi_done, s + 1)
                if s >= 3:
                    pool.wait_ge(hy_done, s - 2)
                pool.tensor_tensor(hlo[0:n, s % 3, :], hact[0:n, s % 3, :],
                                   hhi[0:n, s % 3, :].bitcast(F32), ALU.subtract).then_inc(hlo_done, 1)
                if s == X2T_AT + 1:
                    low_x2(1)

        @block.scalar
        def _(act):
            act.dma_start(w_sb[:, :], w_pack).then_inc(w_in, 16)
            act.dma_start(vec_sb[:, :], vectors.partition_broadcast(128)).then_inc(vec_in, 16)
            act.preload_act_table_set("natural_log_exp_and_others")

            def move_projection(n, bias, proj_done, count, bank_no):
                t, h = PROJ[n]
                act.wait_ge(proj_done, count)
                if n:
                    act.wait_ge(slots_ready, n)
                act.activation(full[:, :], bank(bank_no), ACT.Identity, bias=bias)
                if n >= 2:
                    act.wait_ge(scr_out[t][0], 16)
                act.activation(part[t][:, 0, :], bank(bank_no), ACT.Identity,
                               bias=bias).then_inc(proj_moved, 1)

            def guess_rstd(n, cols):
                act.wait_ge(var_ready, n + 1)
                act.activation(lnv[:, cols], nt[:, 0, cols], ACT.Ln).then_inc(rstd_guess, 1)
                act.wait_ge(rstd_guess, 2 * n + 1)
                act.activation(rstd[:, cols], lnv[:, cols], ACT.Exp, scale=-0.5).then_inc(rstd_guess, 1)

            def move_xnT(h):
                act.wait_ge(xnT_ps, h + 1)
                act.activation(xnT[:, HT * h:HT * h + HT], bank(2 + h), ACT.Copy).then_inc(xnT_ready, 1)

            guess_rstd(0, slice(0, HB))
            act.wait_ge(kp_in, 16)
            move_projection(0, bk_sb, kproj, 1, 0)
            move_xnT(0)
            guess_rstd(1, slice(HB, B))
            move_projection(1, bq_sb, qproj, 1, 4)
            move_xnT(1)
            move_projection(2, bk_sb, kproj, 2, 1)
            move_projection(3, bq_sb, qproj, 2, 5)
            act.dma_start(w13_sb[:, :, :], w13T).then_inc(w13_in, 16)
            act.dma_start(w2_sb[:, 1:NBLK, :],
                          w2T[0:NE * NI, :].rearrange("(k p) n -> p k n", p=128)).then_inc(w2_in, 16)
            act.dma_start(w2_sb[0:NI, 0, :], w2T[NE * NI:NE * NI + NI, :]).then_inc(w2_in, 16)
            act.wait_ge(vec_in, 16)
            act.activation(tg[:, :], gates, ACT.Tanh).then_inc(tanh_ready, 1)
            act.preload_act_table_set("natural_log_exp_and_others")

            def move_maxima(b):
                act.wait_ge(mt_done, b + 1)
                if b >= 2:
                    act.wait_ge(m_in[b % 2], 32 * (b // 2))
                act.activation(mT_sb[:, b % 2, :], mT_ps, ACT.Copy).then_inc(mt_copied, 1)

            def exponentials(b, c):
                act.wait_ge(s2_done, 2 * b + c + 1)
                if b >= 2 and c == 0:
                    act.wait_ge(pv_done, b - 1)
                act.activation(PT[:, b % 2, :, :].rearrange("k (p h) q -> k p h q", p=2)
                               [:, :, 4 * c:4 * c + 4, :].rearrange("k p h q -> k p (h q)"),
                               ps[:, S2B:S2B + 2, :], ACT.Exp, scale=DK ** -0.5).then_inc(exp_done, 1)

            def move_values(b):
                act.wait_ge(pv_done, b + 1)
                if b:
                    act.wait_ge(ot_done, b)
                act.activation(OA[:, :], bank(OB), ACT.Copy).then_inc(oa_ready, 1)

            def move_onT(b):
                act.wait_ge(onT_done, b + 1)
                if b:
                    act.wait_ge(wo_done, b)
                act.activation(onT[:, :], bank(OB, S), ACT.Copy).then_inc(onT_ready, 1)

            def move_x2T(h):
                act.wait_ge(x2T_ps, h + 1)
                act.activation(x2hi[h][:, :], bank(MB), ACT.Copy).then_inc(x2hi_ready, 1)
                if h:
                    act.wait_ge(x2lo_ready, h)
                    act.wait_ge(logit_done, h)
                act.activation(x2T[:, :], bank(MB), ACT.Copy).then_inc(x2T_copied, 1)

            def sigmoid_exp(h):
                act.wait_ge(logit_done, h + 1)
                act.activation(eneg[:, :, :], ps[:, MB, 0:HB * NE].rearrange("p (t e) -> p t e", e=NE),
                               ACT.Exp, scale=-1.0).then_inc(eneg_ready, 1)

            def move_combT(h):
                act.wait_ge(combT_ps, h + 1)
                act.activation(combT[h][:, :], combT_bank, ACT.Copy).then_inc(combT_ready, 1)

            for i in range(B + 3):
                if 1 <= i <= B:
                    move_maxima(i - 1)
                if i == HB + 3:
                    guess_rstd(2, slice(0, HB))
                if i >= 3:
                    move_values(i - 3)
                if i == HB + 4:
                    move_x2T(0)
                if 2 <= i < B + 2:
                    exponentials(i - 2, 0)
                if i >= 3:
                    move_onT(i - 3)
                if 2 <= i < B + 2:
                    exponentials(i - 2, 1)
                if i == HB + 4:
                    sigmoid_exp(0)
            guess_rstd(3, slice(HB, B))

            def silus(s):
                r = rows_of(s % NBLK)
                n = r[1] - r[0]
                act.wait_ge(g_done, s + 1)
                wait_u_read(act, s - 2)
                act.activation(silu[0:n, s % 2, :], ps[0:n, GB + s % 2, :],
                               ACT.Silu).then_inc(silu_done, 1)

            def high_h(s):
                r = rows_of(s % NBLK)
                n = r[1] - r[0]
                act.wait_ge(h_done, s + 1)
                if s >= 3:
                    act.wait_ge(hy_done, s - 2)
                act.activation(hhi[0:n, s % 3, :], hact[0:n, s % 3, :], ACT.Copy).then_inc(hhi_done, 1)

            def move_yT(h):
                act.wait_ge(hy_done, NBLK * (h + 1))
                if h:
                    act.wait_ge(y_ps, h)
                act.activation(yT[:, :], bank(YB), ACT.Copy).then_inc(yT_ready, 1)

            for s in range(2 * NBLK):
                silus(s)
                if s == 0:
                    move_combT(0)
                if s:
                    high_h(s - 1)
                if s == X2T_AT:
                    move_x2T(1)
                if s == LOGITS_AT:
                    sigmoid_exp(1)
                if s == COMBT_AT:
                    move_combT(1)
                if s == NBLK + DOWN_LAG:
                    move_yT(0)
            high_h(2 * NBLK - 1)
            move_yT(1)

        @block.vector
        def _(dve):
            steps = [0]

            def step(ins):
                steps[0] += 1
                ins.then_inc(dve_step, 1)
                dve.wait_ge(dve_step, steps[0])

            dve.memset(KS[0][:, :, :].bitcast(F32), ONES2).then_inc(kones, 1)

            def ln_stats(src, b):
                return dve.bn_stats(stats[:, b, :], src[:, b, :])

            def ln_variance(cols):
                for b in range(cols.start, cols.stop):
                    ins = dve.bn_aggr(mv[:, b, :], stats[:, b, :])
                step(ins)
                dve.tensor_scalar(nt[:, 0, cols], mv[:, cols, 1], EPS, None, ALU.add).then_inc(var_ready, 1)

            def ln_apply(n, src, cols):
                dve.wait_ge(rstd_guess, 2 * n + 2)
                step(dve.tensor_tensor(nt[:, 1, cols], rstd[:, cols], rstd[:, cols], ALU.mult))
                step(dve.scalar_tensor_tensor(nt[:, 2, cols], nt[:, 1, cols], -0.5, nt[:, 0, cols],
                                              ALU.mult, ALU.mult))
                step(dve.scalar_tensor_tensor(nt[:, 1, cols], nt[:, 2, cols], 1.5, rstd[:, cols],
                                              ALU.add, ALU.mult))
                for b in range(cols.start, cols.stop):
                    dve.tensor_scalar(xn_sb[:, b, :], src[:, b, :], mv[:, b, 0:1], nt[:, 1, b:b + 1],
                                      ALU.subtract, ALU.mult).then_inc(xn_ready, 1)

            def split(n):
                t, h = PROJ[n]
                p = part[t]
                dve.wait_ge(proj_moved, n + 1)
                if n:
                    dve.wait_ge(slots_ready, n)
                if t == "q":
                    step(dve.tensor_tensor(rest[:, :], full[:, :], p[:, 0, :], ALU.subtract))
                    dve.tensor_copy(p[:, 1:3, :], p[:, 0:1, :].broadcast_to([128, 2, HT]))
                    step(dve.tensor_copy(p[:, 3, :], rest[:, :]))
                    dve.tensor_copy(p[:, 4, :], p[:, 3, :])
                    last = dve.tensor_tensor(p[:, 5, :], rest[:, :], p[:, 3, :], ALU.subtract)
                else:
                    step(dve.tensor_tensor(rest[:, :], full[:, :], p[:, 0, :], ALU.subtract))
                    step(dve.tensor_copy(p[:, 1, :], rest[:, :]))
                    dve.tensor_copy(p[:, 3:5, :], p[:, 0:2, :])
                    dve.tensor_copy(p[:, 5, :], p[:, 0, :])
                    last = dve.tensor_tensor(p[:, 2, :], rest[:, :], p[:, 1, :], ALU.subtract)
                last.then_inc(slots_ready, 1)

            def move_v(n):
                dve.wait_ge(vproj, n + 1)
                dve.tensor_tensor(
                    v_pad[:, HB * n:HB * n + HB, :, 0:DK],
                    bank(6 + n).rearrange("p (b h d) -> p b h d", b=HB, d=DK),
                    bv_sb.rearrange("p (h d) -> p h d", d=DK).unsqueeze(1)
                    .broadcast_to([128, HB, H, DK]), ALU.add).then_inc(v_ready, 1)

            lo4, hi4 = slice(0, HB), slice(HB, B)

            def ln_all_stats(cols):
                for b in range(cols.start, cols.stop):
                    ins = ln_stats(x_sb, b)
                step(ins)
                ln_variance(cols)

            dve.wait_ge(x0_in, 16)
            ln_all_stats(lo4)
            dve.wait_ge(x1_in, 16)
            ln_all_stats(hi4)
            ln_apply(0, x_sb, lo4)
            split(0)
            ln_apply(1, x_sb, hi4)
            split(1)
            split(2)
            dve.wait_ge(vec_in, 16)
            dve.wait_ge(vpad_ready, 1)
            move_v(0)
            split(3)
            move_v(1)

            def maxima(b, c):
                dve.wait_ge(s1_done, 2 * b + c + 1)
                if b and c == 0:
                    dve.wait_ge(parts_done, b)
                dve.tensor_reduce(negmax[:, :, 4 * c:4 * c + 4],
                                  ps[:, S1B:S1B + 2, :].rearrange("q p (h k) -> q p h k", k=S),
                                  AX_X, ALU.max, negate=True).then_inc(max_read, 1)

            def maxima_parts(b):
                dve.wait_ge(max_read, 2 * b + 2)
                if b:
                    dve.wait_ge(mt_done, b)
                step(dve.tensor_copy(maxpart[:, :, 0, :], negmax[:, :, :]))
                step(dve.tensor_tensor(maxrest[:, :, :], negmax[:, :, :], maxpart[:, :, 0, :],
                                       ALU.subtract))
                step(dve.tensor_copy(maxpart[:, :, 1, :], maxrest[:, :, :]))
                dve.tensor_tensor(maxpart[:, :, 2, :], maxrest[:, :, :], maxpart[:, :, 1, :],
                                  ALU.subtract).then_inc(parts_done, 1)

            def normalize(b):
                o = bank(TB).rearrange("q (h r) -> q h r", r=32)
                dve.wait_ge(ot_done, b + 1)
                if b:
                    dve.wait_ge(on_ready, b)
                step(dve.reciprocal(rden[:, :], o[:, :, DK]))
                if b:
                    dve.wait_ge(onT_done, b)
                dve.tensor_tensor(on_sb[:, :, :], o[:, :, 0:DK],
                                  rden[:, :].unsqueeze(2).broadcast_to([128, H, DK]),
                                  ALU.mult).then_inc(on_ready, 1)

            def residual(b):
                dve.wait_ge(wo_done, b + 1)
                if b == 0:
                    dve.wait_ge(xb_ready, 1)
                dve.scalar_tensor_tensor(x2_sb[:, b, :], bank(YB, D), tg[:, 0:1], xb_sb[:, b, :],
                                         ALU.mult, ALU.add).then_inc(x2_done, 1)
                dve.wait_ge(x2_done, b + 1)
                step(ln_stats(x2_sb, b))

            def route_scores(h):
                dve.wait_ge(eneg_ready, h + 1)
                step(dve.tensor_scalar(eneg[:, :, :], eneg[:, :, :], 1.0, None, ALU.add))
                step(dve.reciprocal(score[:, :, :], eneg[:, :, :]))
                step(dve.tensor_tensor(biased[:, :, :], score[:, :, :],
                                       gb_sb.unsqueeze(1).broadcast_to([128, HB, NE]), ALU.add))
                by_group = biased[:, :, :].rearrange("p t (g e) -> p (t g) e", e=EG)
                dve.tensor_tensor(pairs[:, 0, :, :], by_group[:, :, 0:2], by_group[:, :, 2:4], ALU.max)
                step(dve.tensor_tensor(pairs[:, 1, :, :], by_group[:, :, 0:2], by_group[:, :, 2:4],
                                       ALU.min))
                dve.tensor_tensor(gtop[:, 0, :], pairs[:, 0, :, 0], pairs[:, 0, :, 1], ALU.max)
                dve.tensor_tensor(gtop[:, 1, :], pairs[:, 0, :, 0], pairs[:, 0, :, 1], ALU.min)
                step(dve.tensor_tensor(gtop[:, 2, :], pairs[:, 1, :, 0], pairs[:, 1, :, 1], ALU.max))
                step(dve.tensor_tensor(gtop[:, 3, :], gtop[:, 1, :], gtop[:, 2, :], ALU.max))
                step(dve.tensor_tensor(gtop[:, 4, :], gtop[:, 0, :], gtop[:, 3, :], ALU.add))

            def route_groups():
                gs = gtop[:, 4, :].rearrange("p (t g) -> p t g", g=NG)
                other = gs.unsqueeze(2).broadcast_to([128, HB, NG, NG])
                own = gs.unsqueeze(3).broadcast_to([128, HB, NG, NG])
                dve.tensor_tensor(gcmp[:, 0, :, :, :], other, own, ALU.is_gt)
                step(dve.tensor_tensor(gcmp[:, 1, :, :, :], other, own, ALU.is_equal))
                step(dve.tensor_tensor(gcmp[:, 1, :, :, :], gcmp[:, 1, :, :, :], tri[:, :, :, :], ALU.mult))
                step(dve.tensor_tensor(gcmp[:, 0, :, :, :], gcmp[:, 0, :, :, :], gcmp[:, 1, :, :, :],
                                       ALU.add))
                step(dve.tensor_reduce(gpen[:, 0, :],
                                       gcmp[:, 0, :, :, :].rearrange("p t g o -> p (t g) o"),
                                       AX_X, ALU.add))
                step(dve.tensor_scalar(gpen[:, 1, :], gpen[:, 0, :], TOP_G - 0.5, MASKED,
                                       ALU.is_ge, ALU.mult))
                step(dve.tensor_tensor(
                    masked[:, :, 0:NE].rearrange("p t (g e) -> p t g e", e=EG),
                    biased[:, :, :].rearrange("p t (g e) -> p t g e", e=EG),
                    gpen[:, 1, :].rearrange("p (t g) -> p t g", g=NG).unsqueeze(3)
                    .broadcast_to([128, HB, NG, EG]), ALU.add))

            def route_top():
                for t in range(HB):
                    ins = dve.max(top8[:, t, :], masked[:, t, :])
                step(ins)
                step(dve.memset(top8[:, :, TOP_E:8], SENT))
                for t in range(HB):
                    ins = dve.match_replace(taken[:, t, :], top8[:, t, :], masked[:, t, :], TAKEN)
                step(ins)

            def route_weights(h):
                step(dve.scalar_tensor_tensor(wsel[:, :, :], taken[:, :, 0:NE], TAKEN / 2,
                                              score[:, :, :], ALU.is_ge, ALU.mult))
                step(dve.tensor_reduce(wsum[:, 0, :], wsel[:, :, :], AX_X, ALU.add))
                step(dve.tensor_scalar(wsum[:, 1, :], wsum[:, 0, :], 1e-20, None, ALU.add))
                step(dve.reciprocal(wsum[:, 2, :], wsum[:, 1, :]))
                step(dve.scalar_tensor_tensor(comb[:, :, :], wsel[:, :, :], SCALE,
                                              wsum[:, 2, :].unsqueeze(2).broadcast_to([128, HB, NE]),
                                              ALU.mult, ALU.mult))
                if h:
                    dve.wait_ge(combT_ps, h)
                step(dve.tensor_copy(combpart[:, :, 0, :], comb[:, :, :]))
                step(dve.tensor_tensor(combrest[:, :, :], comb[:, :, :], combpart[:, :, 0, :],
                                       ALU.subtract))
                step(dve.tensor_copy(combpart[:, :, 1, :], combrest[:, :, :]))
                dve.tensor_tensor(combpart[:, :, 2, :], combrest[:, :, :], combpart[:, :, 1, :],
                                  ALU.subtract).then_inc(comb_ready, 1)

            for i in range(B + 3):
                if i < B:
                    maxima(i, 0)
                if i < B:
                    maxima(i, 1)
                if i >= 3:
                    normalize(i - 3)
                if i < B:
                    maxima_parts(i)
                if i >= 3:
                    residual(i - 3)
                if i == HB + 2:
                    ln_variance(lo4)
                if i == HB + 3:
                    dve.wait_ge(xnT_ps, NHALF)
                    ln_apply(2, x2_sb, lo4)
                if i == HB + 4:
                    dve.wait_ge(consts, 2)
                    route_scores(0)
                    route_groups()
                if i == HB + 5:
                    route_top()
                    route_weights(0)
            ln_variance(hi4)
            ln_apply(3, x2_sb, hi4)

            def ffn_step(s):
                k = s % NBLK
                r = rows_of(k)
                n = r[1] - r[0]
                dve.wait_ge(silu_done, s + 1)
                dve.wait_ge(u_done, s + 1)
                if s >= 3:
                    dve.wait_ge(hlo_done, s - 2)
                    dve.wait_ge(hhi_done, s - 2)
                if k == 0:
                    dve.tensor_tensor(hact[0:n, s % 3, :], silu[0:n, s % 2, :], ps[0:n, UB + s % 2, :],
                                      ALU.mult).then_inc(h_done, 1)
                else:
                    if s >= 2:
                        dve.wait_ge(h_done, s - 1)
                    dve.tensor_tensor(su[:, s % 2, :], silu[:, s % 2, :], ps[:, UB + s % 2, :],
                                      ALU.mult).then_inc(u_read, 1)
                    dve.wait_ge(u_read, routed(s))
                    dve.wait_ge(c_done, routed(s))
                    dve.tensor_tensor(hact[:, s % 3, :], su[:, s % 2, :], ps[:, CB + s % 2, :],
                                      ALU.mult).then_inc(h_done, 1)

            def finish(h):
                dve.wait_ge(y_ps, h + 1)
                dve.scalar_tensor_tensor(o_sb[:, HB * h:HB * h + HB, :].rearrange("p b d -> p (b d)"),
                                         bank(MB), tg[:, 1:2],
                                         x2_sb[:, HB * h:HB * h + HB, :].rearrange("p b d -> p (b d)"),
                                         ALU.mult, ALU.add).then_inc(out_ready, 1)

            for s in range(2 * NBLK):
                ffn_step(s)
                if s == LOGITS_AT:
                    route_scores(1)
                if s == LOGITS_AT + 1:
                    route_groups()
                if s == LOGITS_AT + 2:
                    route_top()
                if s == LOGITS_AT + 3:
                    route_weights(1)
                if s == NBLK + DOWN_LAG + 1:
                    finish(0)
            finish(1)

        @block.tensor
        def _(pe):
            def matmul(o, lhsT, rhs, start=True, stop=True):
                return pe.matmul(o, lhsT, rhs, start=start, stop=stop)

            def project_v(n):
                for b in range(HB * n, HB * n + HB):
                    ins = matmul(ps[:, 6 + n, (b % HB) * D:(b % HB + 1) * D],
                                 ctx_sb[n][:, (b % HB) * S:(b % HB + 1) * S], wv_sb)
                ins.then_inc(vproj, 1)

            def transpose_xn(h):
                for b in range(HB * h, HB * h + HB):
                    pe.wait_ge(xn_ready, b + 1)
                    ins = pe.transpose(ps[:, 2 + h, (b % HB) * S:(b % HB + 1) * S], xn_sb[:, b, :],
                                       identF[:, :])
                ins.then_inc(xnT_ps, 1)

            def project_q(h):
                pe.wait_ge(xnT_ready, h + 1)
                matmul(bank(4 + h), wq_sb, xnT[:, HT * h:HT * h + HT]).then_inc(qproj, 1)

            pe.wait_ge(kp_in, 16)
            matmul(bank(0), wk_sb, ctx_sb[0]).then_inc(kproj, 1)
            pe.wait_ge(ident_ready, 1)
            pe.wait_ge(w_in, 16)
            transpose_xn(0)
            project_q(0)
            pe.wait_ge(ctx1_in, 16)
            matmul(bank(1), wk_sb, ctx_sb[1]).then_inc(kproj, 1)
            transpose_xn(1)
            project_q(1)
            project_v(0)
            project_v(1)

            def scores(b, c):
                n = 2 * b + c
                h, ts = tok(b)
                if n == 0:
                    pe.wait_ge(proj_moved, 3)
                if n == 0 or n == 2 * HB:
                    pe.wait_ge(stacked["k"][h], 32)
                    pe.wait_ge(stacked["q"][h], 32)
                if n:
                    pe.wait_ge(max_read, n)
                for i in range(4):
                    for ph in range(2):
                        hp = 4 * c + i
                        rows = slice(64 * ph, 64 * ph + KROWS)
                        ins = matmul(ps[:, S1B + ph, i * S:(i + 1) * S], QS[h][rows, hp, ts],
                                     KS[h][rows, hp, ts])
                ins.then_inc(s1_done, 1)

            def scores_less_max(b, c):
                n = 2 * b + c
                h, ts = tok(b)
                if n == 0:
                    pe.wait_ge(xnT_ready, 2)
                if c == 0:
                    pe.wait_ge(m_in[b % 2], 32 * (b // 2 + 1))
                if n:
                    pe.wait_ge(exp_done, n)
                for i in range(4):
                    for ph in range(2):
                        hp = 4 * c + i
                        rows = slice(64 * ph, 64 * ph + MROWS)
                        ins = matmul(ps[:, S2B + ph, i * S:(i + 1) * S], KS[h][rows, hp, ts],
                                     QS[h][rows, hp, ts])
                ins.then_inc(s2_done, 1)

            def transpose_maxima(b):
                pe.wait_ge(parts_done, b + 1)
                if b == 0:
                    pe.wait_ge(bident_ready, 1)
                    pe.wait_ge(proj_moved, 4)
                else:
                    pe.wait_ge(mt_copied, b)
                if b >= 3:
                    pe.wait_ge(on_ready, b - 2)
                pe.transpose(mT_ps, maxpart[:, :, :, :].rearrange("q p r h -> q (p r h)"),
                             identB[:, :]).then_inc(mt_done, 1)

            def values(b):
                pe.wait_ge(exp_done, 2 * b + 2)
                if b == 0:
                    pe.wait_ge(v_ready, 2)
                else:
                    pe.wait_ge(onT_ready, b)
                for g in range(4):
                    for j in range(4):
                        head = 4 * g + j
                        ins = matmul(ps[32 * j:32 * j + 32, OB, g * S:(g + 1) * S],
                                     v_pad[:, b, head, :], PT[:, b % 2, head, :])
                ins.then_inc(pv_done, 1)

            def transpose_values(b):
                pe.wait_ge(oa_ready, b + 1)
                pe.wait_ge(mt_copied, min(b + 3, B))
                if b:
                    pe.wait_ge(on_ready, b)
                for g in range(4):
                    ins = pe.transpose(ps[:, TB, g * S:(g + 1) * S], OA[:, g * S:(g + 1) * S],
                                       identF[:, :])
                ins.then_inc(ot_done, 1)

            def transpose_normalized(b):
                pe.wait_ge(on_ready, b + 1)
                pe.transpose(bank(OB, S), on_sb[:, :, :].rearrange("q h d -> q (h d)"),
                             identF[:, :]).then_inc(onT_done, 1)

            def project_out(b):
                pe.wait_ge(onT_ready, b + 1)
                if b:
                    pe.wait_ge(x2_done, b)
                matmul(bank(YB, D), onT[:, :], wo_sb).then_inc(wo_done, 1)

            def transpose_x2(h):
                if h:
                    pe.wait_ge(combT_ready, h)
                for b in range(HB * h, HB * h + HB):
                    pe.wait_ge(xn_ready, B + b + 1)
                    ins = pe.transpose(ps[:, MB, (b % HB) * S:(b % HB + 1) * S], xn_sb[:, b, :],
                                       identF[:, :])
                ins.then_inc(x2T_ps, 1)

            def logits(h):
                pe.wait_ge(x2T_copied, h + 1)
                pe.wait_ge(x2hi_ready, h + 1)
                for t in range(HB):
                    ins = matmul(ps[:, MB, t * NE:(t + 1) * NE], x2T[:, t * S:(t + 1) * S], gw_sb)
                ins.then_inc(logit_done, 1)

            def transpose_comb(h):
                pe.wait_ge(comb_ready, h + 1)
                for t in range(HB):
                    ins = pe.transpose(combT_bank[:, t * S:(t + 1) * S],
                                       combpart[:, t, :, :].rearrange("p r e -> p (r e)"), identB[:, :])
                ins.then_inc(combT_ps, 1)

            for i in range(B + 3):
                if i < B:
                    scores(i, 0)
                if 1 <= i <= B:
                    transpose_maxima(i - 1)
                if i >= 3:
                    values(i - 3)
                if i < B:
                    scores(i, 1)
                if i == HB + 4:
                    transpose_x2(0)
                if i >= 3:
                    transpose_values(i - 3)
                if 2 <= i < B + 2:
                    scores_less_max(i - 2, 0)
                if i >= 3:
                    transpose_normalized(i - 3)
                if i == HB + 4:
                    logits(0)
                if 2 <= i < B + 2:
                    scores_less_max(i - 2, 1)
                if i >= 3:
                    project_out(i - 3)

            def split_product(o, whi, wlo, hi, lo, start=True, stop=True):
                matmul(o, whi, hi, start=start, stop=False)
                matmul(o, whi, lo, start=False, stop=False)
                return matmul(o, wlo, hi, start=False, stop=stop)

            def up(s):
                h, k = divmod(s, NBLK)
                r = rows_of(k)
                n = r[1] - r[0]
                cols = slice(*r)
                if k == 0:
                    pe.wait_ge(x2lo_ready, h + 1)
                if s == 0:
                    pe.wait_ge(wsplit, 2)
                if s >= 2:
                    pe.wait_ge(silu_done, s - 1)
                split_product(ps[0:n, GB + s % 2, :], w13hi[:, 0, cols], w13lo[:, 0, cols],
                              x2hi[h][:, :], x2lo[h][:, :]).then_inc(g_done, 1)
                wait_u_read(pe, s - 2)
                split_product(ps[0:n, UB + s % 2, :], w13hi[:, 1, cols], w13lo[:, 1, cols],
                              x2hi[h][:, :], x2lo[h][:, :]).then_inc(u_done, 1)
                if s == 0:
                    transpose_comb(0)
                if k:
                    if k == 1:
                        pe.wait_ge(combT_ready, h + 1)
                    if s == 1:
                        pe.wait_ge(sel_ready, 1)
                    if s >= 2:
                        pe.wait_ge(h_done, s - 1)
                    matmul(ps[:, CB + s % 2, :], sel[:, :, :].rearrange("p e i -> p (e i)")[:, cols],
                           combT[h][:, :]).then_inc(c_done, 1)

            def down(s):
                h, k = divmod(s, NBLK)
                r = rows_of(k)
                n = r[1] - r[0]
                pe.wait_ge(hhi_done, s + 1)
                pe.wait_ge(hlo_done, s + 1)
                if s == 0:
                    pe.wait_ge(wsplit, 3)
                if s == NBLK:
                    pe.wait_ge(yT_ready, 1)
                split_product(bank(YB), w2hi[0:n, k, :], w2lo[0:n, k, :], hhi[0:n, s % 3, :],
                              hlo[0:n, s % 3, :], start=(k == 0), stop=(k == NBLK - 1)).then_inc(hy_done, 1)

            def transpose_y(h):
                pe.wait_ge(yT_ready, h + 1)
                if h:
                    pe.wait_ge(out_ready, h)
                for t in range(HB):
                    ins = pe.transpose(ps[:, MB, t * D:(t + 1) * D], yT[:, t * S:(t + 1) * S],
                                       identF[:, :])
                ins.then_inc(y_ps, 1)

            for s in range(2 * NBLK + DOWN_LAG):
                if s < 2 * NBLK:
                    up(s)
                if s >= DOWN_LAG:
                    down(s - DOWN_LAG)
                if s == X2T_AT:
                    transpose_x2(1)
                if s == LOGITS_AT:
                    logits(1)
                if s == COMBT_AT:
                    transpose_comb(1)
                if s == NBLK + DOWN_LAG + 1:
                    transpose_y(0)
            transpose_y(1)


ONES2 = float(np.array([0x3F803F80], np.uint32).view(np.float32)[0])
DOWN_LAG = 3
X2T_AT, LOGITS_AT, COMBT_AT = 0, 2, 7


def kernel(x, ctx_1024, g_xattn, g_ffn, L0_xattn_Wq, L0_xattn_bq, L0_xattn_Wk, L0_xattn_bk,
           L0_xattn_Wv, L0_xattn_bv, L0_xattn_Wo, L0_xattn_bo, L0_ffn_gate_w, L0_ffn_gate_bias,
           L0_ffn_w1, L0_ffn_w2, L0_ffn_w3, L0_ffn_ws1, L0_ffn_ws2, L0_ffn_ws3):
    import concourse.bacc as bacc
    from concourse.bass_utils import run_bass_kernel_spmd

    def column(a):
        return np.asarray(a).reshape(D, 1)

    def side_by_side(*arrays):
        return np.ascontiguousarray(np.concatenate([np.asarray(a) for a in arrays], -1))

    def features_first(w, shared):
        return np.concatenate([np.asarray(w).reshape(NE * NI, D), np.asarray(shared)], 0).T

    ctxT = np.asarray(ctx_1024).reshape(NT, D).T
    w2 = np.transpose(np.asarray(L0_ffn_w2), (0, 2, 1)).reshape(NE * NI, D)
    w1, w3 = features_first(L0_ffn_w1, L0_ffn_ws1), features_first(L0_ffn_w3, L0_ffn_ws3)
    arrays = {
        "x": np.ascontiguousarray(x),
        "k_pack": side_by_side(np.asarray(L0_xattn_Wk).T, column(L0_xattn_bk), column(L0_xattn_bq),
                               ctxT[:, 0:HT]),
        "ctxT1": side_by_side(ctxT[:, HT:NT]),
        "w_pack": side_by_side(np.asarray(L0_xattn_Wq).T, np.asarray(L0_xattn_Wv).T,
                               np.asarray(L0_xattn_Wo).T, np.asarray(L0_ffn_gate_w).T),
        "vectors": side_by_side(L0_xattn_bv, L0_xattn_bo, L0_ffn_gate_bias, g_xattn, g_ffn),
        "w13T": np.ascontiguousarray(np.stack([w1, w3], 1)),
        "w2T": np.ascontiguousarray(np.concatenate([w2, np.asarray(L0_ffn_ws2).T], 0)),
    }
    nc = bacc.Bacc("TRN2", target_bir_lowering=False, num_devices=1)
    args = [nc.dram_tensor(f"in_{n}", a.shape, mybir.dt.from_np(a.dtype), kind="ExternalInput").ap()
            for n, a in arrays.items()]
    out = nc.dram_tensor("out", (B, S, D), F32, kind="ExternalOutput").ap()
    flamingo(nc, *args, out)
    r = run_bass_kernel_spmd(nc, [{f"in_{n}": a for n, a in arrays.items()}], core_ids=[0])
    return r.results[0]["out"]
```

```python
from contextlib import ExitStack

import numpy as np

import concourse.bass as bass
from concourse import mybir

F32 = mybir.dt.float32
F32R = mybir.dt.float32r
I32 = mybir.dt.int32
BF16 = mybir.dt.bfloat16
ALU = mybir.AluOpType
ACT = mybir.ActivationFunctionType
AX_X = mybir.AxisListType.X

B, S, D = 8, 128, 128
H = 16
DK = D // H
NT = B * S
NHALF = 2
HB = B // NHALF
HT = NT // NHALF
QT = NT // 4
NQ = NT // QT
QB = QT // S
HP = H // 2
NE, NI, NG = 16, 96, 4
EG = NE // NG
TOP_G, TOP_E = 2, 4
SCALE = 2.5
EPS = 1e-5
PARTS = 3
MPARTS = 2
SLOTS = {"q": (0, 0, 0, 1, 1, 2), "k": (0, 1, 2, 0, 1, 0)}
NS = len(SLOTS["q"])
KROWS = NS * DK
MROWS = KROWS + MPARTS
NBLK = NE * NI // 128 + 1
SENT, MASKED, TAKEN = -3e38, -1e38, 3e38


def rows_of(k):
    return (NE * NI, NE * NI + NI) if k == 0 else ((k - 1) * 128, k * 128)


def flamingo(nc, x, k_pack, ctxT1, w_pack, vectors, w13T, w2T, out):
    with ExitStack() as stack:
        def sb(name, shape, dt=F32):
            return stack.enter_context(nc.sbuf_tensor(name, shape, dt))

        def sem(name):
            return stack.enter_context(nc.semaphore(name))

        k_sb = sb("k_sb", [128, D + 2 + QT])
        ctx1_sb = sb("ctx1_sb", [128, NT - QT])
        w_sb = sb("w_sb", [128, 3 * D + NE])
        vec_sb = sb("vec_sb", [128, 2 * D + NE + 2])
        x_sb = sb("x_sb", [128, B, D])
        xb_sb = sb("xb_sb", [128, B, D])
        xn_sb = sb("xn_sb", [128, B, D])
        xnT = sb("xnT", [128, NT])
        x2_sb = sb("x2_sb", [128, B, D])
        wk_sb, bk_sb, bq_sb = k_sb[:, 0:D], k_sb[:, D:D + 1], k_sb[:, D + 1:D + 2]
        wq_sb, wv_sb, wo_sb = w_sb[:, 0:D], w_sb[:, D:2 * D], w_sb[:, 2 * D:3 * D]
        gw_sb = w_sb[:, 3 * D:3 * D + NE]
        bv_sb, bo_sb = vec_sb[:, 0:D], vec_sb[:, D:2 * D]
        gb_sb, gates = vec_sb[:, 2 * D:2 * D + NE], vec_sb[:, 2 * D + NE:2 * D + NE + 2]
        tg = sb("tg", [128, 2])
        w_stage = sb("w_stage", [128, NBLK * D])
        w13hi = sb("w13hi", [128, 2, NE * NI + NI], F32R)
        w13lo = sb("w13lo", [128, 2, NE * NI + NI], F32R)
        w2hi, w2lo = sb("w2hi", [128, NBLK, D], F32R), sb("w2lo", [128, NBLK, D], F32R)
        identF, identB = sb("identF", [128, 128]), sb("identB", [128, 128], BF16)
        rest = sb("rest", [128, 2, QT])
        part = {"q": sb("qpart", [128, 2, NS, QT], BF16), "k": sb("kpart", [128, 2, NS, QT], BF16)}
        QS = [sb(f"QS{h}", [128, HP, 2, HT], BF16) for h in range(NHALF)]
        KS = [sb(f"KS{h}", [128, HP, HT], BF16) for h in range(NHALF)]
        v_pad = sb("v_pad", [128, B, H, 32])
        PT = sb("PT", [128, 2, H, S])
        negmax = sb("negmax", [128, 2, HP])
        maxpart = sb("maxpart", [128, 2, MPARTS, HP], BF16)
        mT_sb = sb("mT_sb", [2 * MPARTS * HP, 2, S], BF16)
        OA = sb("OA", [128, 4 * S])
        rden = sb("rden", [128, H])
        on_sb = sb("on_sb", [128, H, DK])
        onT = sb("onT", [128, S])
        stats = sb("stats", [128, B, 6])
        mv = sb("mv", [128, B, 2])
        lnv, rstd = sb("lnv", [128, B]), sb("rstd", [128, B])
        nt = sb("nt", [128, 3, B])
        x2T = sb("x2T", [128, HT])
        x2hi = [sb(f"x2hi{h}", [128, HT], F32R) for h in range(NHALF)]
        x2lo = [sb(f"x2lo{h}", [128, HT], F32R) for h in range(NHALF)]
        eneg = sb("eneg", [128, HB, NE])
        score = sb("score", [128, HB, NE])
        biased = sb("biased", [128, HB, NE])
        pairs = sb("pairs", [128, 2, HB * NG, 2])
        gtop = sb("gtop", [128, 5, HB * NG])
        gcmp = sb("gcmp", [128, 2, HB, NG, NG])
        tri = sb("tri", [128, HB, NG, NG])
        gpen = sb("gpen", [128, 2, HB * NG])
        masked = sb("masked", [128, HB, NE + TOP_E])
        top8 = sb("top8", [128, HB, 8])
        taken = sb("taken", [128, HB, NE + TOP_E])
        wsel = sb("wsel", [128, HB, NE])
        wsum = sb("wsum", [128, 3, HB])
        comb = sb("comb", [128, HB, NE])
        combrest = sb("combrest", [128, HB, NE])
        combpart = sb("combpart", [128, HB, PARTS, NE], BF16)
        combT = [sb(f"combT{h}", [PARTS * NE, HT], BF16) for h in range(NHALF)]
        sel = sb("sel", [PARTS * NE, NE, NI], BF16)
        products = QS[0][:, :, :, :].bitcast(F32).rearrange("p a b c -> p (a b c)")\
            .rearrange("p (i q) -> p i q", q=HT)
        hact, silu = products[:, 0:HBUF, :], products[:, HBUF:HBUF + 2, :]
        su = KS[0][:, :, :].bitcast(F32).rearrange("p a b -> p (a b)")\
            .rearrange("p (i q) -> p i q", q=HT)
        hhi, hlo = sb("hhi", [128, HBUF, HT], F32R), sb("hlo", [128, HBUF, HT], F32R)
        yT = PT[:, 0, 0:HB, :].rearrange("p h q -> p (h q)")
        o_sb = xb_sb
        scr = {t: [nc.dram_tensor(f"scr_{t}{c}", [H * DK, NS * QT], BF16, kind="Internal").ap()
                   for c in range(NQ)] for t in "qk"}

        ps = stack.enter_context(nc.psum_tensor("ps", [128, 8, 512], F32))

        x0_in, x1_in, kp_in, ctx1_in = sem("x0_in"), sem("x1_in"), sem("kp_in"), sem("ctx1_in")
        w_in, vec_in, w1_in, w3_in, w2_in = (sem("w_in"), sem("vec_in"), sem("w1_in"), sem("w3_in"),
                                             sem("w2_in"))
        ident_ready, bident_ready, consts = sem("ident_ready"), sem("bident_ready"), sem("consts")
        vpad_ready, stack_set = sem("vpad_ready"), [sem(f"stack_set{c}") for c in range(NQ)]
        xb_ready, sel_ready, wsplit = sem("xb_ready"), sem("sel_ready"), sem("wsplit")
        pool_step, dve_step = sem("pool_step"), sem("dve_step")
        tanh_ready = sem("tanh_ready")
        kproj, qproj, vproj = sem("kproj"), sem("qproj"), sem("vproj")
        proj_moved, rest_ready, slots_ready = sem("proj_moved"), sem("rest_ready"), sem("slots_ready")
        whi_ready = sem("whi_ready")
        first_copied, mid_ready, low_ready = sem("first_copied"), sem("mid_ready"), sem("low_ready")
        ln_ready, xn_rest_ready = sem("ln_ready"), sem("xn_rest_ready")
        scr_out = {t: [sem(f"scr_out_{t}{c}") for c in range(NQ)] for t in "qk"}
        stacked = {t: [sem(f"stacked_{t}{c}") for c in range(NQ)] for t in "qk"}
        var_ready, rstd_guess = sem("var_ready"), sem("rstd_guess")
        xn_ready, xnT_ps, xnT_ready = sem("xn_ready"), sem("xnT_ps"), sem("xnT_ready")
        v_ready = sem("v_ready")
        s1_done, max_read = sem("s1_done"), sem("max_read")
        parts_done, mt_done, mt_copied = sem("parts_done"), sem("mt_done"), sem("mt_copied")
        m_in = [sem("m_in0"), sem("m_in1")]
        s2_done, exp_done, pv_done, oa_ready = (sem("s2_done"), sem("exp_done"), sem("pv_done"),
                                                sem("oa_ready"))
        ot_done, on_ready, onT_done, onT_ready = (sem("ot_done"), sem("on_ready"), sem("onT_done"),
                                                  sem("onT_ready"))
        wo_done, x2_done = sem("wo_done"), sem("x2_done")
        x2T_ps, x2T_copied, x2hi_ready, x2lo_ready = (sem("x2T_ps"), sem("x2T_copied"),
                                                      sem("x2hi_ready"), sem("x2lo_ready"))
        logit_done, eneg_ready, comb_ready = sem("logit_done"), sem("eneg_ready"), sem("comb_ready")
        combT_ps, combT_ready = sem("combT_ps"), sem("combT_ready")
        g_done, u_done, c_done = sem("g_done"), sem("u_done"), sem("c_done")
        silu_done, u_read, h_done = sem("silu_done"), sem("u_read"), sem("h_done")
        hhi_done, hlo_done, hy_done = sem("hhi_done"), sem("hlo_done"), sem("hy_done")
        yT_ready, y_ps, out_ready, out_sent = (sem("yT_ready"), sem("y_ps"), sem("out_ready"),
                                               sem("out_sent"))

        block = stack.enter_context(nc.Block())

        S1B, S2B, OB, TB, MB = (0, 6), 2, 4, 5, 7
        YB, TYB = (6, 7), (6, 6, 7)
        GB, UB, CB = (0, 2), (1, 3), (4, 5)
        combT_bank = ps[0:PARTS * NE, MB, 0:HT // 2].bitcast(BF16)

        mT_ps = ps[0:2 * MPARTS * HP, TB, S:S + S // 2].bitcast(BF16)

        def bank(n, cols=512):
            return ps[:, n, 0:cols]

        def set_stacks(eng, c):
            cols = slice(QT * (c % 2) // 2, QT * (c % 2) // 2 + QT // 2)
            eng.memset(KS[c // 2][:, :, :].bitcast(F32)[:, :, cols], ONES2).then_inc(stack_set[c], 1)
            eng.memset(QS[c // 2][:, :, :, :].bitcast(F32)[:, :, :, cols], 0.0)\
                .then_inc(stack_set[c], 1)

        def w13_half(n):
            half = (NE * NI + NI) // 2
            return slice(half * n, half * n + half)

        def ctxT(first, n):
            if first < QT:
                return k_sb[:, D + 2 + first:D + 2 + first + n]
            return ctx1_sb[:, first - QT:first - QT + n]

        def tok(b):
            return b // HB, slice((b % HB) * S, (b % HB + 1) * S)

        def routed(s):
            return s - s // NBLK

        def wait_u_read(eng, s):
            if s >= 0 and s % NBLK:
                eng.wait_ge(u_read, routed(s))
            elif s >= 0:
                eng.wait_ge(h_done, s + 1)

        PROJ = [(t, c) for c in range(NQ) for t in "kq"]
        PROJ_BANK = {("k", 0): 0, ("q", 0): 1, ("k", 1): 4, ("q", 1): 5, ("k", 2): 3, ("q", 2): 4}

        MID, LOW = {"q": (3, 4), "k": (1, 4)}, {"q": 5, "k": 2}

        def proj_ps(t, c):
            cols = slice(QT * (c == 3), QT * (c == 3) + QT)
            return ps[:, PROJ_BANK[t, min(c, 2)], cols]

        def gather(eng, n):
            t, c = PROJ[n]
            cols = slice(QT * (c % 2), QT * (c % 2) + QT)
            eng.wait_ge(scr_out[t][c], 16)
            eng.wait_ge(stack_set[c], 2)
            for ph in range(2):
                src = scr[t][c][HP * DK * ph:HP * DK * (ph + 1), :]
                rows = slice(64 * ph, 64 * ph + KROWS)
                eng.dma_start(QS[c // 2][rows, :, ph, cols] if t == "q" else KS[c // 2][rows, :, cols],
                              src.rearrange("(h d) (s t) -> (d s) h t", d=DK, s=NS)
                              ).then_inc(stacked[t][c], 16)

        def send_out(eng, n):
            batches = slice(OUT_BATCHES[n].start, OUT_BATCHES[n].stop)
            eng.dma_start(out[batches].rearrange("b s d -> s b d"),
                          o_sb[:, batches, :]).then_inc(out_sent, 16)

        @block.sync
        def _(sp):
            sp.dma_start(x_sb[:, 0:QB, :], x[0:QB].rearrange("b s d -> s b d")).then_inc(x0_in, 16)
            sp.dma_start(k_sb[:, :], k_pack).then_inc(kp_in, 16)
            sp.dma_start(x_sb[:, QB:B, :], x[QB:B].rearrange("b s d -> s b d")).then_inc(x1_in, 16)
            sp.dma_start(ctx1_sb[:, :], ctxT1).then_inc(ctx1_in, 16)

            def spread(n):
                t, c = PROJ[n]
                if n < SPLIT_BY_DVE:
                    sp.wait_ge(slots_ready, n + 1)
                else:
                    sp.wait_ge(low_ready, n - SPLIT_BY_DVE + 1)
                sp.wait_ge(first_copied, n + 1)
                sp.dma_start(scr[t][c], part[t][:, c % 2, :, :].rearrange("p s t -> p (s t)"))\
                    .then_inc(scr_out[t][c], 16)

            spread(0)
            spread(1)
            gather(sp, 0)
            spread(2)
            gather(sp, 1)
            spread(3)
            gather(sp, 2)
            gather(sp, 3)
            spread(4)
            spread(5)
            for b in range(B):
                h, ts = tok(b)
                sp.wait_ge(mt_copied, b + 1)
                for ph in range(2):
                    n = MPARTS * HP
                    sp.dma_start(QS[h][64 * ph + KROWS:64 * ph + MROWS, :, ph, ts],
                                 mT_sb[n * ph:n * ph + n, b % 2, :]).then_inc(m_in[b % 2], 16)
                if b == 0:
                    gather(sp, 4)
                    spread(6)
                    gather(sp, 5)
                if b == 1:
                    spread(7)
                    gather(sp, 6)
                if b == 2:
                    gather(sp, 7)
            for n in range(2):
                sp.wait_ge(out_ready, n + 1)
                send_out(sp, n)
            sp.wait_ge(out_sent, 16 * len(OUT_BATCHES))

        @block.gpsimd
        def _(pool):
            steps = [0]

            def step(ins):
                steps[0] += 1
                ins.then_inc(pool_step, 1)
                pool.wait_ge(pool_step, steps[0])

            step(pool.memset(identF[:, :], 0.0))
            pool.affine_select(out=identF[:, :], in_=identF[:, :], compare_op=ALU.not_equal, fill=1.0,
                               base=0, pattern=[[-1, 128]], channel_multiplier=1).then_inc(ident_ready, 1)
            pool.wait_ge(ident_ready, 1)
            pool.tensor_copy(identB[:, :], identF[:, :]).then_inc(bident_ready, 1)
            set_stacks(pool, 1)
            step(pool.memset(v_pad[:, :, :, :], 0.0))
            pool.memset(v_pad[:, :, :, DK:DK + 1], 1.0).then_inc(vpad_ready, 1)
            pool.wait_ge(ln_ready, 1)
            for b in range(2 * QB, B):
                pool.tensor_scalar(xn_sb[:, b, :], x_sb[:, b, :], mv[:, b, 0:1], nt[:, 1, b:b + 1],
                                   ALU.subtract, ALU.mult).then_inc(xn_rest_ready, 1)
            for c in range(2, NQ):
                set_stacks(pool, c)
            for n in range(SPLIT_BY_DVE, len(PROJ)):
                t, c = PROJ[n]
                pool.wait_ge(mid_ready, n - SPLIT_BY_DVE + 1)
                pool.tensor_tensor(part[t][:, c % 2, LOW[t], :], rest[:, n % 2, :],
                                   part[t][:, c % 2, MID[t][0], :], ALU.subtract).then_inc(low_ready, 1)
            pool.memset(masked[:, :, NE:NE + TOP_E], SENT).then_inc(consts, 1)
            step(pool.memset(tri[:, :, :, :], 1.0))
            pool.affine_select(out=tri[:, :, :, :], in_=tri[:, :, :, :], compare_op=ALU.is_gt, fill=0.0,
                               base=0, pattern=[[0, HB], [1, NG], [-1, NG]],
                               channel_multiplier=0).then_inc(consts, 1)
            for i in range(2):
                for part_no in range(2):
                    cols = w13_half(part_no)
                    pool.wait_ge(whi_ready, 2 * i + part_no + 1)
                    pool.tensor_tensor(w13lo[:, i, cols], w_stage[:, cols],
                                       w13hi[:, i, cols].bitcast(F32),
                                       ALU.subtract).then_inc(wsplit, 1)
                pool.wait_ge(wsplit, 2 * i + 2)
                if i == 0:
                    pool.dma_start(w_stage[:, 0:NE * NI + NI], w13T[:, 1, :]).then_inc(w3_in, 16)
                    pool.wait_ge(vec_in, 16)
                    pool.wait_ge(tanh_ready, 1)
                    step(pool.tensor_scalar(bo_sb, bo_sb, tg[:, 0:1], None, ALU.mult))
                    pool.wait_ge(x0_in, 16)
                    pool.wait_ge(x1_in, 16)
                    pool.tensor_tensor(xb_sb[:, :, :], x_sb[:, :, :],
                                       bo_sb.unsqueeze(1).broadcast_to([128, B, D]),
                                       ALU.add).then_inc(xb_ready, 1)
                else:
                    pool.dma_start(w_stage[:, D:NBLK * D].rearrange("p (k n) -> p k n", n=D),
                                   w2T[0:NE * NI, :].rearrange("(k p) n -> p k n", p=128)
                                   ).then_inc(w2_in, 16)
                    pool.dma_start(w_stage[0:NI, 0:D],
                                   w2T[NE * NI:NE * NI + NI, :]).then_inc(w2_in, 16)
            step(pool.memset(sel[:, :, :], 0.0))
            for p in range(PARTS):
                ins = pool.affine_select(out=sel[:, :, :], in_=sel[:, :, :], compare_op=ALU.not_equal,
                                         fill=1.0, base=-NE * p, pattern=[[-1, NE], [0, NI]],
                                         channel_multiplier=1)
                if p < PARTS - 1:
                    step(ins)
                else:
                    ins.then_inc(sel_ready, 1)
            def low_x2(h):
                pool.wait_ge(x2T_copied, h + 1)
                pool.wait_ge(x2hi_ready, h + 1)
                pool.tensor_tensor(x2lo[h][:, :], x2T[:, :], x2hi[h][:, :].bitcast(F32),
                                   ALU.subtract).then_inc(x2lo_ready, 1)

            low_x2(0)
            pool.wait_ge(whi_ready, 6)
            w2_sb = w_stage[:, :].rearrange("p (k n) -> p k n", n=D)
            pool.tensor_tensor(w2lo[0:NI, 0, :], w2_sb[0:NI, 0, :], w2hi[0:NI, 0, :].bitcast(F32),
                               ALU.subtract)
            pool.tensor_tensor(w2lo[:, 1:NBLK, :], w2_sb[:, 1:NBLK, :],
                               w2hi[:, 1:NBLK, :].bitcast(F32), ALU.subtract).then_inc(wsplit, 1)

            for s in range(2 * NBLK - 2):
                r = rows_of(s % NBLK)
                n = r[1] - r[0]
                pool.wait_ge(hhi_done, s + 1)
                if s >= HBUF:
                    pool.wait_ge(hy_done, s + 1 - HBUF)
                pool.tensor_tensor(hlo[0:n, s % HBUF, :], hact[0:n, s % HBUF, :],
                                   hhi[0:n, s % HBUF, :].bitcast(F32), ALU.subtract).then_inc(hlo_done, 1)
                if s == X2T_AT - 1:
                    low_x2(1)

        @block.scalar
        def _(act):
            act.dma_start(w_sb[:, :], w_pack).then_inc(w_in, 16)
            act.dma_start(vec_sb[:, :], vectors.partition_broadcast(128)).then_inc(vec_in, 16)
            act.preload_act_table_set("natural_log_exp_and_others")

            def first_part(n):
                t, c = PROJ[n]
                act.wait_ge(kproj if t == "k" else qproj, min(c, 2) + 1)
                if c >= 2:
                    act.wait_ge(scr_out[t][c - 2], 16)
                if c == 3:
                    act.wait_ge(rest_ready, n - 1)
                act.activation(part[t][:, c % 2, 0, :], proj_ps(t, c), ACT.Identity,
                               bias=bk_sb if t == "k" else bq_sb).then_inc(proj_moved, 1)

            def copy_first_part(n):
                t, c = PROJ[n]
                to = slice(1, 3) if t == "q" else slice(3, 6, 2)
                act.wait_ge(proj_moved, n + 1)
                act.activation(part[t][:, c % 2, to, :],
                               part[t][:, c % 2, 0:1, :].broadcast_to([128, 2, QT]),
                               ACT.Copy).then_inc(first_copied, 1)

            def second_part(n):
                t, c = PROJ[n]
                one, other = MID[t]
                act.wait_ge(rest_ready, n + 1)
                act.activation(part[t][:, c % 2, one:other + 1:other - one, :],
                               rest[:, n % 2, :].unsqueeze(1).broadcast_to([128, 2, QT]),
                               ACT.Copy).then_inc(mid_ready, 1)

            def guess_rstd(n, cols):
                act.wait_ge(var_ready, n + 1)
                act.activation(lnv[:, cols], nt[:, 0, cols], ACT.Ln).then_inc(rstd_guess, 1)
                act.wait_ge(rstd_guess, 2 * n + 1)
                act.activation(rstd[:, cols], lnv[:, cols], ACT.Exp, scale=-0.5).then_inc(rstd_guess, 1)

            def move_xnT(n):
                cols = XN_COLS[n]
                act.wait_ge(xnT_ps, n + 1)
                act.activation(xnT[:, cols], bank(2 + n % 2, cols.stop - cols.start),
                               ACT.Copy).then_inc(xnT_ready, 1)

            guess_rstd(0, slice(0, QB))
            act.dma_start(w_stage[:, 0:NE * NI + NI], w13T[:, 0, :]).then_inc(w1_in, 16)
            act.wait_ge(kp_in, 16)
            first_part(0)
            copy_first_part(0)
            move_xnT(0)
            guess_rstd(1, slice(QB, B))
            first_part(1)
            first_part(2)
            copy_first_part(1)
            act.preload_act_table_set("exp_and_others")
            act.wait_ge(vec_in, 16)
            act.activation(tg[:, :], gates, ACT.Tanh).then_inc(tanh_ready, 1)
            move_xnT(1)
            copy_first_part(2)
            first_part(3)
            copy_first_part(3)
            move_xnT(2)
            for n in range(SPLIT_BY_DVE, len(PROJ) - 1):
                first_part(n)
                copy_first_part(n)
                if n < 6:
                    second_part(n)

            def high_weights(i, part_no):
                if i < 2:
                    act.wait_ge((w1_in, w3_in)[i], 16)
                    cols = w13_half(part_no)
                    ins = act.activation(w13hi[:, i, cols], w_stage[:, cols], ACT.Copy)
                elif part_no == 0:
                    act.wait_ge(w2_in, 32)
                    act.activation(w2hi[0:NI, 0, :], w_stage[0:NI, 0:D], ACT.Copy)
                    ins = act.activation(w2hi[:, 1:7, :].rearrange("p k n -> p (k n)"),
                                         w_stage[:, D:7 * D], ACT.Copy)
                else:
                    ins = act.activation(w2hi[:, 7:NBLK, :].rearrange("p k n -> p (k n)"),
                                         w_stage[:, 7 * D:NBLK * D], ACT.Copy)
                ins.then_inc(whi_ready, 1)

            def move_maxima(b):
                act.wait_ge(mt_done, b + 1)
                if b >= 2:
                    act.wait_ge(m_in[b % 2], 32 * (b // 2))
                act.activation(mT_sb[:, b % 2, :], mT_ps, ACT.Copy).then_inc(mt_copied, 1)

            def exponentials(b, c):
                act.wait_ge(s2_done, 2 * b + c + 1)
                if b >= 2 and c == 0:
                    act.wait_ge(pv_done, b - 1)
                act.activation(PT[:, b % 2, :, :].rearrange("k (p h) q -> k h p q", p=2)
                               [:, 4 * c:4 * c + 4, :, :],
                               ps[:, S2B:S2B + 2, :].rearrange("k n (h p q) -> k n h p q", h=2, p=2)
                               .rearrange("k n h p q -> k (n h) p q"), ACT.Exp, scale=DK ** -0.5).then_inc(exp_done, 1)

            def move_values(b):
                act.wait_ge(pv_done, b + 1)
                if b:
                    act.wait_ge(ot_done, b)
                act.activation(OA[:, :], bank(OB), ACT.Copy).then_inc(oa_ready, 1)

            def move_onT(b):
                act.wait_ge(onT_done, b + 1)
                act.wait_ge(mt_done, min(b + 4, B))
                if b:
                    act.wait_ge(wo_done, b)
                act.activation(onT[:, :], bank(TB, S), ACT.Copy).then_inc(onT_ready, 1)

            def move_x2T(h):
                act.wait_ge(x2T_ps, h + 1)
                if h:
                    act.wait_ge(x2lo_ready, h)
                    act.wait_ge(logit_done, h)
                act.activation(x2T[:, :], bank(MB), ACT.Copy).then_inc(x2T_copied, 1)
                act.activation(x2hi[h][:, :], bank(MB), ACT.Copy).then_inc(x2hi_ready, 1)

            def sigmoid_exp(h):
                act.wait_ge(logit_done, h + 1)
                act.activation(eneg[:, :, :], ps[:, MB, 0:HB * NE].rearrange("p (t e) -> p t e", e=NE),
                               ACT.Exp, scale=-1.0).then_inc(eneg_ready, 1)

            def move_combT(h):
                act.wait_ge(combT_ps, h + 1)
                act.activation(combT[h][:, :], combT_bank, ACT.Copy).then_inc(combT_ready, 1)

            def silus(s):
                r = rows_of(s % NBLK)
                n = r[1] - r[0]
                act.wait_ge(g_done, s + 1)
                wait_u_read(act, s - 2)
                act.activation(silu[0:n, s % 2, :], ps[0:n, GB[s % 2], :],
                               ACT.Silu).then_inc(silu_done, 1)

            def high_h(s):
                r = rows_of(s % NBLK)
                n = r[1] - r[0]
                act.wait_ge(h_done, s + 1)
                if s >= HBUF:
                    act.wait_ge(hy_done, s + 1 - HBUF)
                act.activation(hhi[0:n, s % HBUF, :], hact[0:n, s % HBUF, :], ACT.Copy).then_inc(hhi_done, 1)

            def move_yT(n):
                batches = OUT_BATCHES[n]
                h = batches.start // HB
                cols = slice((batches.start - HB * h) * S, (batches.stop - HB * h) * S)
                act.wait_ge(hy_done, NBLK * (h + 1))
                if h:
                    act.wait_ge(y_ps, 1)
                act.activation(yT[:, cols], ps[:, YB[h], cols], ACT.Copy).then_inc(yT_ready, 1)

            for i in range(B):
                if i >= 4:
                    move_onT(i - 4)
                if i:
                    move_maxima(i - 1)
                if i == 1:
                    first_part(7)
                    copy_first_part(7)
                    second_part(6)
                    second_part(7)
                if i == 2:
                    high_weights(0, 0)
                    high_weights(0, 1)
                if i >= 2:
                    exponentials(i - 2, 0)
                if i >= 3:
                    move_values(i - 3)
                if i >= 2:
                    exponentials(i - 2, 1)
                if i in (4, 5):
                    high_weights(1, i - 4)
                if i == B - 1:
                    guess_rstd(2, slice(0, HB))
                    high_weights(2, 0)
                if i == HB + 2:
                    act.preload_act_table_set("natural_log_exp_and_others")
            move_onT(B - 4)
            move_maxima(B - 1)
            exponentials(B - 2, 0)
            move_values(B - 3)
            exponentials(B - 2, 1)
            move_x2T(0)
            high_weights(2, 1)
            move_onT(B - 3)
            exponentials(B - 1, 0)
            sigmoid_exp(0)
            move_values(B - 2)
            exponentials(B - 1, 1)
            move_onT(B - 2)
            move_values(B - 1)
            silus(0)
            move_onT(B - 1)
            silus(1)
            high_h(0)
            for s in range(2, EARLY):
                silus(s)
                if s == EARLY - 2:
                    move_combT(0)

            for s in range(EARLY, 2 * NBLK):
                if s == EARLY:
                    for early in range(1, EARLY - 2):
                        high_h(early)
                if s == COMBT_AT:
                    move_combT(1)
                silus(s)
                if s == X2T_AT:
                    move_x2T(1)
                high_h(s - 2)
                if s == LOGITS_AT - 1:
                    sigmoid_exp(1)
                if s == NBLK + DOWN_LAG + 1:
                    move_yT(0)
            high_h(2 * NBLK - 2)
            high_h(2 * NBLK - 1)
            move_yT(1)
            move_yT(2)
            act.wait_ge(out_ready, 3)
            send_out(act, 2)

        @block.vector
        def _(dve):
            steps = [0]

            def step(ins):
                steps[0] += 1
                ins.then_inc(dve_step, 1)
                dve.wait_ge(dve_step, steps[0])

            def mark(ins):
                steps[0] += 1
                ins.then_inc(dve_step, 1)

            set_stacks(dve, 0)

            def ln_stats(src, b):
                return dve.bn_stats(stats[:, b, :], src[:, b, :])

            def ln_variance(cols):
                for b in range(cols.start, cols.stop):
                    ins = dve.bn_aggr(mv[:, b, :], stats[:, b, :])
                step(ins)
                dve.tensor_scalar(nt[:, 0, cols], mv[:, cols, 1], EPS, None, ALU.add).then_inc(var_ready, 1)

            def newton_step(to, r, cols):
                step(dve.tensor_tensor(nt[:, 2, cols], r, r, ALU.mult))
                step(dve.scalar_tensor_tensor(nt[:, 2, cols], nt[:, 2, cols], -0.5, nt[:, 0, cols],
                                              ALU.mult, ALU.mult))
                step(dve.scalar_tensor_tensor(to, nt[:, 2, cols], 1.5, r, ALU.add, ALU.mult))

            def ln_refine(n, cols, for_pool=None):
                dve.wait_ge(rstd_guess, 2 * n + 2)
                newton_step(nt[:, 1, cols], rstd[:, cols], cols)
                if for_pool:
                    dve.tensor_copy(nt[:, 2, cols], nt[:, 1, cols]).then_inc(for_pool, 1)

            def ln_apply(src, cols):
                for b in range(cols.start, cols.stop):
                    dve.tensor_scalar(xn_sb[:, b, :], src[:, b, :], mv[:, b, 0:1], nt[:, 1, b:b + 1],
                                      ALU.subtract, ALU.mult).then_inc(xn_ready, 1)

            def split(n):
                t, c = PROJ[n]
                p, left = part[t][:, c % 2, :, :], rest[:, n % 2, :]
                dve.wait_ge(proj_moved, n + 1)
                if n >= SPLIT_BY_DVE + 2:
                    dve.wait_ge(low_ready, n - SPLIT_BY_DVE - 1)
                elif n >= 2:
                    dve.wait_ge(slots_ready, n - 1)
                dve.scalar_tensor_tensor(left, proj_ps(t, c), bk_sb if t == "k" else bq_sb,
                                         p[:, 0, :], ALU.add, ALU.subtract).then_inc(rest_ready, 1)
                if n < SPLIT_BY_DVE:
                    one, other = MID[t]
                    dve.wait_ge(rest_ready, n + 1)
                    step(dve.tensor_copy(p[:, one, :], left))
                    dve.tensor_copy(p[:, other, :], p[:, one, :])
                    dve.tensor_tensor(p[:, LOW[t], :], left, p[:, one, :],
                                      ALU.subtract).then_inc(slots_ready, 1)

            def move_v(n):
                dve.wait_ge(vproj, n + 1)
                dve.tensor_tensor(
                    v_pad[:, HB * n:HB * n + HB, :, 0:DK],
                    bank((TB, OB)[n]).rearrange("p (b h d) -> p b h d", b=HB, d=DK),
                    bv_sb.rearrange("p (h d) -> p h d", d=DK).unsqueeze(1)
                    .broadcast_to([128, HB, H, DK]), ALU.add).then_inc(v_ready, 1)

            lo4, hi4 = slice(0, HB), slice(HB, B)

            def ln_all_stats(cols):
                for b in range(cols.start, cols.stop):
                    ins = ln_stats(x_sb, b)
                step(ins)
                ln_variance(cols)

            dve.wait_ge(x0_in, 16)
            ln_all_stats(slice(0, QB))
            ln_refine(0, slice(0, QB))
            ln_apply(x_sb, slice(0, QB))
            dve.wait_ge(x1_in, 16)
            ln_all_stats(slice(QB, B))
            dve.wait_ge(kp_in, 16)
            split(0)
            split(1)
            ln_refine(1, slice(QB, B), ln_ready)
            ln_apply(x_sb, slice(QB, 2 * QB))
            split(2)
            split(3)
            split(4)

            def maxima(b, c):
                dve.wait_ge(s1_done, 2 * b + c + 1)
                if b and c == 0:
                    dve.wait_ge(parts_done, b)
                dve.tensor_reduce(negmax[:, :, 4 * c:4 * c + 4],
                                  ps[:, S1B[c]:S1B[c] + 2, :].rearrange("q p (h k) -> q p h k", k=S),
                                  AX_X, ALU.max, negate=True).then_inc(max_read, 1)

            def maxima_parts(b):
                dve.wait_ge(max_read, 2 * b + 2)
                if b:
                    dve.wait_ge(mt_done, b)
                mark(dve.tensor_copy(maxpart[:, :, 0, :], negmax[:, :, :]))
                if b >= 4:
                    dve.wait_ge(x2_done, b - 3)
                    mark(ln_stats(x2_sb, b - 4))
                dve.wait_ge(dve_step, steps[0] - (b >= 4))
                dve.tensor_tensor(maxpart[:, :, 1, :], negmax[:, :, :], maxpart[:, :, 0, :],
                                  ALU.subtract).then_inc(parts_done, 1)

            def normalize(b):
                o = bank(TB).rearrange("q (h r) -> q h r", r=32)
                dve.wait_ge(ot_done, b + 1)
                if b:
                    dve.wait_ge(on_ready, b)
                step(dve.reciprocal(rden[:, :], o[:, :, DK]))
                if b:
                    dve.wait_ge(onT_done, b)
                dve.tensor_tensor(on_sb[:, :, :], o[:, :, 0:DK],
                                  rden[:, :].unsqueeze(2).broadcast_to([128, H, DK]),
                                  ALU.mult).then_inc(on_ready, 1)

            def residual(b):
                dve.wait_ge(wo_done, b + 1)
                if b == 0:
                    dve.wait_ge(xb_ready, 1)
                dve.scalar_tensor_tensor(x2_sb[:, b, :], bank(TB, D), tg[:, 0:1], xb_sb[:, b, :],
                                         ALU.mult, ALU.add).then_inc(x2_done, 1)

            def route_scores(h):
                dve.wait_ge(eneg_ready, h + 1)
                step(dve.tensor_scalar(eneg[:, :, :], eneg[:, :, :], 1.0, None, ALU.add))
                step(dve.reciprocal(score[:, :, :], eneg[:, :, :]))
                step(dve.tensor_tensor(biased[:, :, :], score[:, :, :],
                                       gb_sb.unsqueeze(1).broadcast_to([128, HB, NE]), ALU.add))

            def route_pairs():
                by_group = biased[:, :, :].rearrange("p t (g e) -> p (t g) e", e=EG)
                dve.tensor_tensor(pairs[:, 0, :, :], by_group[:, :, 0:2], by_group[:, :, 2:4], ALU.max)
                step(dve.tensor_tensor(pairs[:, 1, :, :], by_group[:, :, 0:2], by_group[:, :, 2:4],
                                       ALU.min))
                dve.tensor_tensor(gtop[:, 0, :], pairs[:, 0, :, 0], pairs[:, 0, :, 1], ALU.max)
                dve.tensor_tensor(gtop[:, 1, :], pairs[:, 0, :, 0], pairs[:, 0, :, 1], ALU.min)
                step(dve.tensor_tensor(gtop[:, 2, :], pairs[:, 1, :, 0], pairs[:, 1, :, 1], ALU.max))
                step(dve.tensor_tensor(gtop[:, 3, :], gtop[:, 1, :], gtop[:, 2, :], ALU.max))
                step(dve.tensor_tensor(gtop[:, 4, :], gtop[:, 0, :], gtop[:, 3, :], ALU.add))

            def route_groups():
                gs = gtop[:, 4, :].rearrange("p (t g) -> p t g", g=NG)
                other = gs.unsqueeze(2).broadcast_to([128, HB, NG, NG])
                own = gs.unsqueeze(3).broadcast_to([128, HB, NG, NG])
                dve.tensor_tensor(gcmp[:, 0, :, :, :], other, own, ALU.is_gt)
                step(dve.tensor_tensor(gcmp[:, 1, :, :, :], other, own, ALU.is_equal))
                step(dve.tensor_tensor(gcmp[:, 1, :, :, :], gcmp[:, 1, :, :, :], tri[:, :, :, :], ALU.mult))
                step(dve.tensor_tensor(gcmp[:, 0, :, :, :], gcmp[:, 0, :, :, :], gcmp[:, 1, :, :, :],
                                       ALU.add))
                step(dve.tensor_reduce(gpen[:, 0, :],
                                       gcmp[:, 0, :, :, :].rearrange("p t g o -> p (t g) o"),
                                       AX_X, ALU.add))
                step(dve.tensor_scalar(gpen[:, 1, :], gpen[:, 0, :], TOP_G - 0.5, MASKED,
                                       ALU.is_ge, ALU.mult))
                step(dve.tensor_tensor(
                    masked[:, :, 0:NE].rearrange("p t (g e) -> p t g e", e=EG),
                    biased[:, :, :].rearrange("p t (g e) -> p t g e", e=EG),
                    gpen[:, 1, :].rearrange("p (t g) -> p t g", g=NG).unsqueeze(3)
                    .broadcast_to([128, HB, NG, EG]), ALU.add))

            def route_top():
                for t in range(HB):
                    ins = dve.max(top8[:, t, :], masked[:, t, :])
                step(ins)
                step(dve.memset(top8[:, :, TOP_E:8], SENT))
                for t in range(HB):
                    ins = dve.match_replace(taken[:, t, :], top8[:, t, :], masked[:, t, :], TAKEN)
                step(ins)

            def route_sums():
                step(dve.scalar_tensor_tensor(wsel[:, :, :], taken[:, :, 0:NE], TAKEN / 2,
                                              score[:, :, :], ALU.is_ge, ALU.mult))
                step(dve.tensor_reduce(wsum[:, 0, :], wsel[:, :, :], AX_X, ALU.add))

            def route_weights():
                step(dve.tensor_scalar(wsum[:, 1, :], wsum[:, 0, :], 1e-20, None, ALU.add))
                step(dve.reciprocal(wsum[:, 2, :], wsum[:, 1, :]))
                step(dve.scalar_tensor_tensor(comb[:, :, :], wsel[:, :, :], SCALE,
                                              wsum[:, 2, :].unsqueeze(2).broadcast_to([128, HB, NE]),
                                              ALU.mult, ALU.mult))

            def route_parts(h):
                if h:
                    dve.wait_ge(combT_ps, h)
                step(dve.tensor_copy(combpart[:, :, 0, :], comb[:, :, :]))
                step(dve.tensor_tensor(combrest[:, :, :], comb[:, :, :], combpart[:, :, 0, :],
                                       ALU.subtract))
                step(dve.tensor_copy(combpart[:, :, 1, :], combrest[:, :, :]))
                dve.tensor_tensor(combpart[:, :, 2, :], combrest[:, :, :], combpart[:, :, 1, :],
                                  ALU.subtract).then_inc(comb_ready, 1)

            def times_u(s):
                if s % NBLK:
                    dve.wait_ge(silu_done, s + 1)
                    dve.wait_ge(u_done, s + 1)
                    if s >= 4:
                        dve.wait_ge(h_done, s - 3)
                    dve.tensor_tensor(su[:, s % 4, :], silu[:, s % 2, :], ps[:, UB[s % 2], :],
                                      ALU.mult).then_inc(u_read, 1)

            def times_weight(s):
                if s >= HBUF:
                    dve.wait_ge(hlo_done, s + 1 - HBUF)
                    dve.wait_ge(hhi_done, s + 1 - HBUF)
                if s % NBLK == 0:
                    dve.wait_ge(silu_done, s + 1)
                    dve.wait_ge(u_done, s + 1)
                    dve.tensor_tensor(hact[0:NI, s % HBUF, :], silu[0:NI, s % 2, :],
                                      ps[0:NI, UB[s % 2], :], ALU.mult).then_inc(h_done, 1)
                else:
                    dve.wait_ge(u_read, routed(s))
                    dve.wait_ge(c_done, routed(s))
                    dve.tensor_tensor(hact[:, s % HBUF, :], su[:, s % 4, :], ps[:, CB[s % 2], :],
                                      ALU.mult).then_inc(h_done, 1)

            def finish(n):
                batches = slice(OUT_BATCHES[n].start, OUT_BATCHES[n].stop)
                dve.wait_ge(y_ps, n + 1)
                dve.scalar_tensor_tensor(o_sb[:, batches, :].rearrange("p b d -> p (b d)"),
                                         bank(TYB[n], len(OUT_BATCHES[n]) * D), tg[:, 1:2],
                                         x2_sb[:, batches, :].rearrange("p b d -> p (b d)"),
                                         ALU.mult, ALU.add).then_inc(out_ready, 1)

            for i in range(B):
                if i >= 4:
                    normalize(i - 4)
                maxima(i, 0)
                if i == 1:
                    split(6)
                maxima(i, 1)
                if i >= 4:
                    residual(i - 4)
                maxima_parts(i)
                if i == B - 1:
                    dve.wait_ge(dve_step, steps[0])
                    ln_variance(lo4)
                if i == 2:
                    move_v(1)
                if i == 0:
                    split(5)
                    dve.wait_ge(vec_in, 16)
                    dve.wait_ge(vpad_ready, 1)
                    move_v(0)
                if i == 1:
                    split(7)
            normalize(B - 4)
            ln_refine(2, lo4)
            dve.wait_ge(xnT_ps, len(XN_COLS))
            ln_apply(x2_sb, lo4)
            residual(B - 4)
            normalize(B - 3)
            residual(B - 3)
            route_scores(0)
            normalize(B - 2)
            route_pairs()
            dve.wait_ge(consts, 2)
            route_groups()
            residual(B - 2)
            route_top()
            normalize(B - 1)
            times_weight(0)
            times_u(1)
            route_sums()
            times_u(2)
            route_weights()
            route_parts(0)
            residual(B - 1)
            times_u(3)
            dve.wait_ge(x2_done, B)
            for b in range(HB, B):
                mark(ln_stats(x2_sb, b))
            times_weight(1)
            dve.wait_ge(dve_step, steps[0])
            ln_variance(hi4)
            root = (nt[:, 1, hi4], rstd[:, hi4])
            dve.wait_ge(var_ready, 4)
            mark(dve.tensor_scalar(root[1].bitcast(I32), nt[:, 0, hi4].bitcast(I32),
                                   -0.5, RSQRT_BITS, ALU.mult, ALU.add))
            for s in range(EARLY - 1, 2 * NBLK):
                times_u(s)
                if s == EARLY - 1:
                    times_weight(s - 2)
                if s != NBLK + 1:
                    times_weight(s - 1)
                if s == EARLY:
                    dve.wait_ge(dve_step, steps[0])
                    newton_step(root[0], root[1], hi4)
                    newton_step(root[1], root[0], hi4)
                    newton_step(root[0], root[1], hi4)
                if s == EARLY + 1:
                    ln_apply(x2_sb, hi4)
                if s == LOGITS_AT - 1:
                    route_scores(1)
                    route_pairs()
                if s == LOGITS_AT:
                    route_groups()
                if s == LOGITS_AT + 1:
                    route_top()
                if s == LOGITS_AT + 2:
                    route_sums()
                    route_weights()
                if s == LOGITS_AT + 3:
                    route_parts(1)
                if s == NBLK:
                    times_weight(s)
                if s == NBLK + DOWN_LAG + 3:
                    finish(0)
            times_weight(2 * NBLK - 1)
            for s in range(2 * NBLK - 2, 2 * NBLK):
                dve.wait_ge(hhi_done, s + 1)
                dve.wait_ge(hlo_done, s)
                dve.wait_ge(hy_done, s + 1 - HBUF)
                dve.tensor_tensor(hlo[:, s % HBUF, :], hact[:, s % HBUF, :],
                                  hhi[:, s % HBUF, :].bitcast(F32), ALU.subtract).then_inc(hlo_done, 1)
            finish(1)
            finish(2)

        @block.tensor
        def _(pe):
            def matmul(o, lhsT, rhs, start=True, stop=True):
                return pe.matmul(o, lhsT, rhs, start=start, stop=stop)

            def project_v(n):
                pe.wait_ge(rest_ready, (4, len(PROJ))[n])
                for b in range(HB * n, HB * n + HB):
                    ins = matmul(ps[:, (TB, OB)[n], (b % HB) * D:(b % HB + 1) * D], ctxT(b * S, S), wv_sb)
                ins.then_inc(vproj, 1)

            def transpose_xn(n):
                cols = XN_COLS[n]
                if n == 2:
                    pe.wait_ge(xnT_ready, 1)
                for b in range(cols.start // S, cols.stop // S):
                    if b < 2 * QB:
                        pe.wait_ge(xn_ready, b + 1)
                    else:
                        pe.wait_ge(xn_rest_ready, b - 2 * QB + 1)
                    at = b * S - cols.start
                    ins = pe.transpose(ps[:, 2 + n % 2, at:at + S], xn_sb[:, b, :], identF[:, :])
                ins.then_inc(xnT_ps, 1)

            def project_k(n):
                cols = XN_COLS[n]
                if n == 1:
                    pe.wait_ge(ctx1_in, 16)
                if n == 2:
                    pe.wait_ge(xnT_ready, 2)
                matmul(bank(PROJ_BANK["k", n], cols.stop - cols.start), wk_sb,
                       ctxT(cols.start, cols.stop - cols.start)).then_inc(kproj, 1)

            def project_q(n):
                cols = XN_COLS[n]
                pe.wait_ge(xnT_ready, n + 1)
                if n == 2:
                    pe.wait_ge(rest_ready, 3)
                matmul(bank(PROJ_BANK["q", n], cols.stop - cols.start), wq_sb,
                       xnT[:, cols]).then_inc(qproj, 1)

            pe.wait_ge(kp_in, 16)
            project_k(0)
            pe.wait_ge(ident_ready, 1)
            pe.wait_ge(w_in, 16)
            transpose_xn(0)
            project_q(0)
            project_k(1)
            transpose_xn(1)
            project_q(1)
            project_k(2)
            transpose_xn(2)

            def scores(b, c):
                n = 2 * b + c
                h, ts = tok(b)
                if c == 0 and b % QB == 0:
                    pe.wait_ge(stacked["k"][b // QB], 32)
                    pe.wait_ge(stacked["q"][b // QB], 32)
                if n >= 2:
                    pe.wait_ge(max_read, n - 1)
                for i in range(4):
                    for ph in range(2):
                        hp = 4 * c + i
                        ins = matmul(ps[:, S1B[c] + ph, i * S:(i + 1) * S], QS[h][:, hp, ph, ts],
                                     KS[h][:, hp, ts])
                ins.then_inc(s1_done, 1)

            def scores_less_max(b, c):
                n = 2 * b + c
                h, ts = tok(b)
                if c == 0:
                    pe.wait_ge(m_in[b % 2], 32 * (b // 2 + 1))
                if n:
                    pe.wait_ge(exp_done, n)
                else:
                    pe.wait_ge(rest_ready, 7)
                for i in range(4):
                    hp = 4 * c + i
                    ins = matmul(ps[:, S2B + i // 2, 2 * S * (i % 2):2 * S * (i % 2) + 2 * S],
                                 KS[h][:, hp, ts], QS[h][:, hp, :, ts])
                ins.then_inc(s2_done, 1)

            def transpose_maxima(b):
                pe.wait_ge(parts_done, b + 1)
                if b == 0:
                    pe.wait_ge(bident_ready, 1)
                    pe.wait_ge(v_ready, 1)
                else:
                    pe.wait_ge(mt_copied, b)
                pe.transpose(mT_ps, maxpart[:, :, :, :].rearrange("q p r h -> q (p r h)"),
                             identB[:, :]).then_inc(mt_done, 1)

            def values(b):
                pe.wait_ge(exp_done, 2 * b + 2)
                if b == 0:
                    pe.wait_ge(v_ready, 2)
                else:
                    pe.wait_ge(oa_ready, b)
                for g in range(4):
                    for j in range(4):
                        head = 4 * g + j
                        ins = matmul(ps[32 * j:32 * j + 32, OB, g * S:(g + 1) * S],
                                     v_pad[:, b, head, :], PT[:, b % 2, head, :])
                ins.then_inc(pv_done, 1)

            def transpose_values(b):
                pe.wait_ge(oa_ready, b + 1)
                if b:
                    pe.wait_ge(x2_done, b)
                else:
                    pe.wait_ge(mt_copied, 3)
                for g in range(4):
                    ins = pe.transpose(ps[:, TB, g * S:(g + 1) * S], OA[:, g * S:(g + 1) * S],
                                       identF[:, :])
                ins.then_inc(ot_done, 1)

            def transpose_normalized(b):
                pe.wait_ge(on_ready, b + 1)
                pe.transpose(bank(TB, S), on_sb[:, :, :].rearrange("q h d -> q (h d)"),
                             identF[:, :]).then_inc(onT_done, 1)

            def project_out(b):
                pe.wait_ge(onT_ready, b + 1)
                pe.wait_ge(mt_copied, min(b + 4, B))
                matmul(bank(TB, D), onT[:, :], wo_sb).then_inc(wo_done, 1)

            def transpose_x2(h):
                if h:
                    pe.wait_ge(combT_ready, h)
                else:
                    pe.wait_ge(max_read, 2 * B)
                for b in range(HB * h, HB * h + HB):
                    pe.wait_ge(xn_ready, 2 * QB + b + 1)
                    ins = pe.transpose(ps[:, MB, (b % HB) * S:(b % HB + 1) * S], xn_sb[:, b, :],
                                       identF[:, :])
                ins.then_inc(x2T_ps, 1)

            def logits(h):
                pe.wait_ge(x2T_copied, h + 1)
                pe.wait_ge(x2hi_ready, h + 1)
                for t in range(HB):
                    ins = matmul(ps[:, MB, t * NE:(t + 1) * NE], x2T[:, t * S:(t + 1) * S], gw_sb)
                ins.then_inc(logit_done, 1)

            def transpose_comb(h):
                pe.wait_ge(comb_ready, h + 1)
                for t in range(HB):
                    ins = pe.transpose(combT_bank[:, t * S:(t + 1) * S],
                                       combpart[:, t, :, :].rearrange("p r e -> p (r e)"), identB[:, :])
                ins.then_inc(combT_ps, 1)

            def split_product(o, whi, wlo, hi, lo, start=True, stop=True):
                matmul(o, whi, hi, start=start, stop=False)
                matmul(o, whi, lo, start=False, stop=False)
                return matmul(o, wlo, hi, start=False, stop=stop)

            def up_g(s):
                h, k = divmod(s, NBLK)
                r = rows_of(k)
                n = r[1] - r[0]
                cols = slice(*r)
                if k == 0:
                    pe.wait_ge(x2lo_ready, h + 1)
                if s == 0:
                    pe.wait_ge(wsplit, 4)
                    pe.wait_ge(max_read, 2 * B)
                if s == 1:
                    pe.wait_ge(exp_done, 2 * B)
                if s >= 2:
                    pe.wait_ge(silu_done, s - 1)
                split_product(ps[0:n, GB[s % 2], :], w13hi[:, 0, cols], w13lo[:, 0, cols],
                              x2hi[h][:, :], x2lo[h][:, :]).then_inc(g_done, 1)

            def up_u(s):
                h, k = divmod(s, NBLK)
                r = rows_of(k)
                n = r[1] - r[0]
                cols = slice(*r)
                wait_u_read(pe, s - 2)
                split_product(ps[0:n, UB[s % 2], :], w13hi[:, 1, cols], w13lo[:, 1, cols],
                              x2hi[h][:, :], x2lo[h][:, :]).then_inc(u_done, 1)

            def up(s):
                up_g(s)
                up_u(s)

            def weights(s):
                h, k = divmod(s, NBLK)
                cols = slice(*rows_of(k))
                if k:
                    if k == 1:
                        pe.wait_ge(combT_ready, h + 1)
                    if s == 1:
                        pe.wait_ge(sel_ready, 1)
                    if s == 1:
                        pe.wait_ge(x2_done, B)
                    if s == 2:
                        pe.wait_ge(oa_ready, B)
                    if s >= 2:
                        pe.wait_ge(h_done, s - 1)
                    matmul(ps[:, CB[s % 2], :], sel[:, :, :].rearrange("p e i -> p (e i)")[:, cols],
                           combT[h][:, :]).then_inc(c_done, 1)

            def down(s):
                h, k = divmod(s, NBLK)
                r = rows_of(k)
                n = r[1] - r[0]
                if s == 0:
                    pe.wait_ge(wsplit, 5)
                if s == NBLK:
                    pe.wait_ge(combT_ready, NHALF)
                pe.wait_ge(hhi_done, s + 1)
                matmul(bank(YB[h]), w2hi[0:n, k, :], hhi[0:n, s % HBUF, :], start=(k == 0), stop=False)
                matmul(bank(YB[h]), w2lo[0:n, k, :], hhi[0:n, s % HBUF, :], start=False, stop=False)
                pe.wait_ge(hlo_done, s + 1)
                matmul(bank(YB[h]), w2hi[0:n, k, :], hlo[0:n, s % HBUF, :], start=False,
                       stop=(k == NBLK - 1)).then_inc(hy_done, 1)

            def transpose_y(n):
                pe.wait_ge(yT_ready, n + 1)
                for t, b in enumerate(OUT_BATCHES[n]):
                    ins = pe.transpose(ps[:, TYB[n], t * D:(t + 1) * D],
                                       yT[:, (b % HB) * S:(b % HB + 1) * S], identF[:, :])
                ins.then_inc(y_ps, 1)

            scores(0, 0)
            for i in range(B):
                if i and i < 4:
                    transpose_maxima(i - 1)
                scores(i, 1)
                if i == 0:
                    project_q(2)
                    project_v(0)
                if i == 2:
                    project_v(1)
                if i in (2, 3):
                    scores_less_max(i - 2, 0)
                if i >= 4:
                    transpose_normalized(i - 4)
                    transpose_maxima(i - 1)
                    scores_less_max(i - 2, 0)
                if i >= 3:
                    values(i - 3)
                if i >= 4:
                    project_out(i - 4)
                if i >= 2:
                    scores_less_max(i - 2, 1)
                if i + 1 < B:
                    scores(i + 1, 0)
                if i >= 3:
                    transpose_values(i - 3)
            transpose_normalized(B - 4)
            transpose_maxima(B - 1)
            scores_less_max(B - 2, 0)
            values(B - 3)
            project_out(B - 4)
            scores_less_max(B - 2, 1)
            transpose_x2(0)
            transpose_values(B - 3)
            scores_less_max(B - 1, 0)
            logits(0)
            transpose_normalized(B - 3)
            values(B - 2)
            project_out(B - 3)
            scores_less_max(B - 1, 1)
            transpose_values(B - 2)
            up_g(0)
            transpose_normalized(B - 2)
            up_u(0)
            values(B - 1)
            project_out(B - 2)
            up_g(1)
            transpose_values(B - 1)
            up_u(1)
            transpose_normalized(B - 1)
            for s in range(2, EARLY - 1):
                up(s)
                if s == 2:
                    project_out(B - 1)
                if s == EARLY - 2:
                    up(EARLY - 1)
            transpose_comb(0)
            down(0)
            weights(1)
            weights(2)

            for s in range(EARLY, 2 * NBLK + DOWN_LAG):
                if s < 2 * NBLK:
                    up_g(s)
                    if s == X2T_AT:
                        transpose_x2(1)
                    if s == LOGITS_AT:
                        logits(1)
                    if s == COMBT_AT:
                        transpose_comb(1)
                    up_u(s)
                if s <= EARLY + 1:
                    weights(s - 2)
                elif s < 2 * NBLK:
                    weights(s - 1)
                if s == 2 * NBLK - 1:
                    weights(s)
                if s > EARLY:
                    down(s - DOWN_LAG - (s == EARLY + 1))
                if s == EARLY + 1:
                    weights(s - 1)
                    down(s - DOWN_LAG)
                if s == NBLK + DOWN_LAG + 2:
                    transpose_y(0)
            pe.wait_ge(out_ready, 1)
            transpose_y(1)
            transpose_y(2)


ONES2 = float(np.array([0x3F803F80], np.uint32).view(np.float32)[0])
RSQRT_BITS = float(0x5F3759DF)
XN_COLS = (slice(0, QT), slice(QT, 2 * QT), slice(2 * QT, NT))
SPLIT_BY_DVE = 4
OUT_BATCHES = (range(0, HB), range(HB, HB + QB), range(HB + QB, B))
DOWN_LAG = 4
HBUF = 4
X2T_AT, LOGITS_AT, COMBT_AT = 8, 9, 15
EARLY = 5


def kernel(x, ctx_1024, g_xattn, g_ffn, L0_xattn_Wq, L0_xattn_bq, L0_xattn_Wk, L0_xattn_bk,
           L0_xattn_Wv, L0_xattn_bv, L0_xattn_Wo, L0_xattn_bo, L0_ffn_gate_w, L0_ffn_gate_bias,
           L0_ffn_w1, L0_ffn_w2, L0_ffn_w3, L0_ffn_ws1, L0_ffn_ws2, L0_ffn_ws3):
    import concourse.bacc as bacc
    from concourse.bass_utils import run_bass_kernel_spmd

    def column(a):
        return np.asarray(a).reshape(D, 1)

    def side_by_side(*arrays):
        return np.ascontiguousarray(np.concatenate([np.asarray(a) for a in arrays], -1))

    def features_first(w, shared):
        return np.concatenate([np.asarray(w).reshape(NE * NI, D), np.asarray(shared)], 0).T

    ctxT = np.asarray(ctx_1024).reshape(NT, D).T
    w2 = np.transpose(np.asarray(L0_ffn_w2), (0, 2, 1)).reshape(NE * NI, D)
    w1, w3 = features_first(L0_ffn_w1, L0_ffn_ws1), features_first(L0_ffn_w3, L0_ffn_ws3)
    arrays = {
        "x": np.ascontiguousarray(x),
        "k_pack": side_by_side(np.asarray(L0_xattn_Wk).T, column(L0_xattn_bk), column(L0_xattn_bq),
                               ctxT[:, 0:QT]),
        "ctxT1": side_by_side(ctxT[:, QT:NT]),
        "w_pack": side_by_side(np.asarray(L0_xattn_Wq).T, np.asarray(L0_xattn_Wv).T,
                               np.asarray(L0_xattn_Wo).T, np.asarray(L0_ffn_gate_w).T),
        "vectors": side_by_side(L0_xattn_bv, L0_xattn_bo, L0_ffn_gate_bias, g_xattn, g_ffn),
        "w13T": np.ascontiguousarray(np.stack([w1, w3], 1)),
        "w2T": np.ascontiguousarray(np.concatenate([w2, np.asarray(L0_ffn_ws2).T], 0)),
    }
    nc = bacc.Bacc("TRN2", target_bir_lowering=False, num_devices=1)
    args = [nc.dram_tensor(f"in_{n}", a.shape, mybir.dt.from_np(a.dtype), kind="ExternalInput").ap()
            for n, a in arrays.items()]
    out = nc.dram_tensor("out", (B, S, D), F32, kind="ExternalOutput").ap()
    flamingo(nc, *args, out)
    r = run_bass_kernel_spmd(nc, [{f"in_{n}": a for n, a in arrays.items()}], core_ids=[0])
    return r.results[0]["out"]
```
